# Optimizing a Trainium2 kernel written in Bass

```python
import numpy as np
import jax
import jax.numpy as jnp

def _softmax(x, axis=-1):
    return jax.nn.softmax(x, axis=axis)

def _gelu(x):
    return jax.nn.gelu(x, approximate=True)

def _silu(x):
    return jax.nn.silu(x)

def _sigmoid(x):
    return jax.nn.sigmoid(x)

def _layernorm(x, axis=-1, eps=1e-05):
    m = jnp.mean(x, axis=axis, keepdims=True)
    v = jnp.var(x, axis=axis, keepdims=True)
    return (x - m) / jnp.sqrt(v + eps)

def _scatter_add(tgt, idx, src, axis=0):
    return tgt.at[idx].add(src)

def _segment_sum(src, seg, n):
    return jax.ops.segment_sum(src, seg, n)
kernel_name = 'mk_macaron_d1_jaxref_r8_588b0c'

def setup_inputs(seed: int=0):
    np.random.seed(seed)
    _w = jnp.asarray

    def _L0_attn_setup():
        import jax, jax.numpy as jnp
        import numpy as np
        N_LAYERS = 2
        D_MODEL = 128
        D_INNER = 2 * D_MODEL
        D_STATE = 16
        D_CONV = 4
        DT_RANK = D_MODEL // 16
        B_SZ, L = (1, 256)
        EPS = 1e-05

        def layernorm(x, w, b):
            mu = jnp.mean(x, axis=-1, keepdims=True)
            var = jnp.mean(jnp.square(x - mu), axis=-1, keepdims=True)
            return (x - mu) * jax.lax.rsqrt(var + EPS) * w + b

        def mamba(x, in_w, cw, cb, xp_w, dtp_w, dtp_b, A_log, Dp, out_w):
            Bn, Ln, _ = x.shape
            xz = jnp.einsum('bld,ed->ble', x, in_w)
            xc, z = jnp.split(xz, 2, axis=-1)
            xp = jnp.pad(xc, ((0, 0), (D_CONV - 1, 0), (0, 0)))
            xc = sum((xp[:, k:k + Ln, :] * cw[:, k] for k in range(D_CONV))) + cb
            xc = jax.nn.silu(xc)
            dbl = jnp.einsum('ble,re->blr', xc, xp_w)
            dt, Bm, Cm = jnp.split(dbl, [DT_RANK, DT_RANK + D_STATE], axis=-1)
            dt = jax.nn.softplus(jnp.einsum('blr,er->ble', dt, dtp_w) + dtp_b)
            A = -jnp.exp(A_log)
            dA = jnp.exp(dt[..., None] * A)
            dBu = (dt * xc)[..., None] * Bm[:, :, None, :]

            def step(h, inp):
                dA_t, dBu_t, C_t = inp
                h = dA_t * h + dBu_t
                y = jnp.einsum('ben,bn->be', h, C_t)
                return (h, y)
            h0 = jnp.zeros((Bn, D_INNER, D_STATE), dA.dtype)
            _, ys = jax.lax.scan(step, h0, (dA.transpose(1, 0, 2, 3), dBu.transpose(1, 0, 2, 3), Cm.transpose(1, 0, 2)))
            y = ys.transpose(1, 0, 2) + xc * Dp
            y = y * jax.nn.silu(z)
            return jnp.einsum('ble,de->bld', y, out_w)
        key = jax.random.key(seed)
        ks = jax.random.split(key, 12)
        s = 0.02
        dt_init = np.log(np.expm1(0.01)).astype(np.float32)
        A_row = jnp.log(jnp.arange(1, D_STATE + 1, dtype=jnp.float32))
        return {'x': jax.random.normal(ks[0], (B_SZ, L, D_MODEL), jnp.float32), 'ln_w': jnp.ones((N_LAYERS, D_MODEL), jnp.float32), 'ln_b': jnp.zeros((N_LAYERS, D_MODEL), jnp.float32), 'in_proj_w': jax.random.normal(ks[1], (N_LAYERS, 2 * D_INNER, D_MODEL)) * s, 'conv_w': jax.random.normal(ks[2], (N_LAYERS, D_INNER, D_CONV)) * 0.2, 'conv_b': jnp.zeros((N_LAYERS, D_INNER), jnp.float32), 'x_proj_w': jax.random.normal(ks[3], (N_LAYERS, DT_RANK + 2 * D_STATE, D_INNER)) * s, 'dt_proj_w': jax.random.normal(ks[4], (N_LAYERS, D_INNER, DT_RANK)) * DT_RANK ** (-0.5), 'dt_proj_b': jnp.full((N_LAYERS, D_INNER), dt_init), 'A_log': jnp.broadcast_to(A_row, (N_LAYERS, D_INNER, D_STATE)).copy(), 'D_skip': jnp.ones((N_LAYERS, D_INNER), jnp.float32), 'out_proj_w': jax.random.normal(ks[5], (N_LAYERS, D_MODEL, D_INNER)) * s, 'norm_f_w': jnp.ones((D_MODEL,), jnp.float32), 'norm_f_b': jnp.zeros((D_MODEL,), jnp.float32)}
    _L0_attn_in = _L0_attn_setup()

    def _L0_ffn_setup():
        import jax, jax.numpy as jnp
        import numpy as np
        import math
        E = 32
        K = 2
        CF = 1.2
        D = 128
        F = 512
        key = jax.random.key(seed)
        ks = jax.random.split(key, 7)
        s = 0.02
        return {'x': jax.random.normal(ks[0], (4, 256, D), jnp.float32), 'gate_w': jax.random.normal(ks[1], (D, E), jnp.float32) * s, 'gate_b': jnp.zeros((E,), jnp.float32), 'w1': jax.random.normal(ks[2], (E, D, F), jnp.float32) * s, 'b1': jnp.zeros((E, F), jnp.float32), 'w2': jax.random.normal(ks[3], (E, F, D), jnp.float32) * s, 'b2': jnp.zeros((E, D), jnp.float32)}
    _L0_ffn_in = _L0_ffn_setup()
    _d = {'L0_attn_x': _L0_attn_in['x'], 'L0_attn_ln_w': _L0_attn_in['ln_w'], 'L0_attn_ln_b': _L0_attn_in['ln_b'], 'L0_attn_in_proj_w': _L0_attn_in['in_proj_w'], 'L0_attn_conv_w': _L0_attn_in['conv_w'], 'L0_attn_conv_b': _L0_attn_in['conv_b'], 'L0_attn_x_proj_w': _L0_attn_in['x_proj_w'], 'L0_attn_dt_proj_w': _L0_attn_in['dt_proj_w'], 'L0_attn_dt_proj_b': _L0_attn_in['dt_proj_b'], 'L0_attn_A_log': _L0_attn_in['A_log'], 'L0_attn_D_skip': _L0_attn_in['D_skip'], 'L0_attn_out_proj_w': _L0_attn_in['out_proj_w'], 'L0_attn_norm_f_w': _L0_attn_in['norm_f_w'], 'L0_attn_norm_f_b': _L0_attn_in['norm_f_b'], 'L0_ffn_gate_w': _L0_ffn_in['gate_w'], 'L0_ffn_gate_b': _L0_ffn_in['gate_b'], 'L0_ffn_w1': _L0_ffn_in['w1'], 'L0_ffn_b1': _L0_ffn_in['b1'], 'L0_ffn_w2': _L0_ffn_in['w2'], 'L0_ffn_b2': _L0_ffn_in['b2']}
    _x0 = _d['L0_attn_x']
    _d['L0_attn_x'] = jax.random.normal(jax.random.fold_in(jax.random.key(seed), 1), (16, 512, 128), dtype=_x0.dtype)
    del _x0
    return _d

def reference(L0_attn_x, L0_attn_ln_w, L0_attn_ln_b, L0_attn_in_proj_w, L0_attn_conv_w, L0_attn_conv_b, L0_attn_x_proj_w, L0_attn_dt_proj_w, L0_attn_dt_proj_b, L0_attn_A_log, L0_attn_D_skip, L0_attn_out_proj_w, L0_attn_norm_f_w, L0_attn_norm_f_b, L0_ffn_gate_w, L0_ffn_gate_b, L0_ffn_w1, L0_ffn_b1, L0_ffn_w2, L0_ffn_b2):

    def _L0_attn_ref(x, ln_w, ln_b, in_proj_w, conv_w, conv_b, x_proj_w, dt_proj_w, dt_proj_b, A_log, D_skip, out_proj_w, norm_f_w, norm_f_b):
        import jax, jax.numpy as jnp
        import numpy as np
        N_LAYERS = 2
        D_MODEL = 128
        D_INNER = 2 * D_MODEL
        D_STATE = 16
        D_CONV = 4
        DT_RANK = D_MODEL // 16
        B_SZ, L = (1, 256)
        EPS = 1e-05

        def layernorm(x, w, b):
            mu = jnp.mean(x, axis=-1, keepdims=True)
            var = jnp.mean(jnp.square(x - mu), axis=-1, keepdims=True)
            return (x - mu) * jax.lax.rsqrt(var + EPS) * w + b

        def mamba(x, in_w, cw, cb, xp_w, dtp_w, dtp_b, A_log, Dp, out_w):
            Bn, Ln, _ = x.shape
            xz = jnp.einsum('bld,ed->ble', x, in_w)
            xc, z = jnp.split(xz, 2, axis=-1)
            xp = jnp.pad(xc, ((0, 0), (D_CONV - 1, 0), (0, 0)))
            xc = sum((xp[:, k:k + Ln, :] * cw[:, k] for k in range(D_CONV))) + cb
            xc = jax.nn.silu(xc)
            dbl = jnp.einsum('ble,re->blr', xc, xp_w)
            dt, Bm, Cm = jnp.split(dbl, [DT_RANK, DT_RANK + D_STATE], axis=-1)
            dt = jax.nn.softplus(jnp.einsum('blr,er->ble', dt, dtp_w) + dtp_b)
            A = -jnp.exp(A_log)
            dA = jnp.exp(dt[..., None] * A)
            dBu = (dt * xc)[..., None] * Bm[:, :, None, :]

            def step(h, inp):
                dA_t, dBu_t, C_t = inp
                h = dA_t * h + dBu_t
                y = jnp.einsum('ben,bn->be', h, C_t)
                return (h, y)
            h0 = jnp.zeros((Bn, D_INNER, D_STATE), dA.dtype)
            _, ys = jax.lax.scan(step, h0, (dA.transpose(1, 0, 2, 3), dBu.transpose(1, 0, 2, 3), Cm.transpose(1, 0, 2)))
            y = ys.transpose(1, 0, 2) + xc * Dp
            y = y * jax.nn.silu(z)
            return jnp.einsum('ble,de->bld', y, out_w)
        for i in range(N_LAYERS):
            h = layernorm(x, ln_w[i], ln_b[i])
            h = mamba(h, in_proj_w[i], conv_w[i], conv_b[i], x_proj_w[i], dt_proj_w[i], dt_proj_b[i], A_log[i], D_skip[i], out_proj_w[i])
            x = h + x
        return layernorm(x, norm_f_w, norm_f_b)

    def _L0_ffn_ref(x, gate_w, gate_b, w1, b1, w2, b2):
        import jax, jax.numpy as jnp
        import numpy as np
        import math
        E = 32
        K = 2
        CF = 1.2
        D = 128
        F = 512
        orig_shape = x.shape
        xt = x.reshape(-1, D)
        T = xt.shape[0]
        C = int(math.ceil(T * K / E * CF))
        logits = xt @ gate_w + gate_b
        probs = jax.nn.softmax(logits, axis=-1)
        top_w, top_i = jax.lax.top_k(probs, K)
        w = top_w / jnp.sum(top_w, axis=-1, keepdims=True)
        flat_e = top_i.reshape(-1)
        oh = jax.nn.one_hot(flat_e, E, dtype=jnp.int32)
        pos_all = jnp.cumsum(oh, axis=0) - 1
        pos = jnp.take_along_axis(pos_all, flat_e[:, None], axis=1)[:, 0]
        valid = pos < C
        pos_d = jnp.where(valid, pos, C)
        x_rep = jnp.repeat(xt, K, axis=0)
        xe = jnp.zeros((E, C, D), x.dtype).at[flat_e, pos_d].add(x_rep, mode='drop')
        he = jax.nn.gelu(jnp.einsum('ecd,edf->ecf', xe, w1) + b1[:, None, :], approximate=False)
        ye = jnp.einsum('ecf,efd->ecd', he, w2) + b2[:, None, :]
        y_flat = ye[flat_e, jnp.minimum(pos, C - 1)] * valid[:, None].astype(x.dtype)
        y = (y_flat.reshape(T, K, D) * w[..., None]).sum(axis=1)
        return y.reshape(orig_shape)
    x = L0_attn_x
    x = x + 0.5 * _L0_ffn_ref(_layernorm(x, axis=-1), L0_ffn_gate_w, L0_ffn_gate_b, L0_ffn_w1, L0_ffn_b1, L0_ffn_w2, L0_ffn_b2)
    x = x + _L0_attn_ref(_layernorm(x, axis=-1), L0_attn_ln_w, L0_attn_ln_b, L0_attn_in_proj_w, L0_attn_conv_w, L0_attn_conv_b, L0_attn_x_proj_w, L0_attn_dt_proj_w, L0_attn_dt_proj_b, L0_attn_A_log, L0_attn_D_skip, L0_attn_out_proj_w, L0_attn_norm_f_w, L0_attn_norm_f_b)
    x = x + 0.5 * _L0_ffn_ref(_layernorm(x, axis=-1), L0_ffn_gate_w, L0_ffn_gate_b, L0_ffn_w1, L0_ffn_b1, L0_ffn_w2, L0_ffn_b2)
    return x

_drawn_inputs = setup_inputs


def setup_inputs(seed=0):
    import zlib

    import numpy as np

    out = dict(_drawn_inputs(seed))
    spreads = {'L0_attn_ln_w': (1.0, 0.6),
     'L0_attn_ln_b': (0.0, 0.8),
     'L0_attn_conv_b': (0.0, 0.8),
     'L0_attn_dt_proj_b': (-4.600165843963623, 0.6),
     'L0_attn_D_skip': (1.0, 0.6),
     'L0_attn_norm_f_w': (1.0, 0.2),
     'L0_attn_norm_f_b': (0.0, 0.1),
     'L0_ffn_gate_b': (0.0, 0.1),
     'L0_ffn_b1': (0.0, 0.758),
     'L0_ffn_b2': (0.0, 0.1)}
    factors = {'L0_attn_in_proj_w': 8.0,
     'L0_attn_conv_w': 8.0,
     'L0_attn_x_proj_w': 8.0,
     'L0_attn_dt_proj_w': 8.0,
     'L0_attn_A_log': 8.0,
     'L0_attn_out_proj_w': 8.0}
    for name, (base, spread) in spreads.items():
        noise = np.random.default_rng([zlib.crc32(name.encode()), seed]).standard_normal(out[name].shape)
        drawn = base * np.exp(spread * noise) if base else spread * noise
        out[name] = jnp.asarray(drawn.astype(out[name].dtype))
    for name, factor in factors.items():
        out[name] = (out[name] * factor).astype(out[name].dtype)
    return out
```

```python
import concourse.bass as bass
from concourse import mybir
from contextlib import ExitStack

F32 = mybir.dt.float32
BF16 = mybir.dt.bfloat16
I32 = mybir.dt.int32
U32 = mybir.dt.uint32
ALU = mybir.AluOpType
ACT = mybir.ActivationFunctionType
AX_X = mybir.AxisListType.X

P = 128
EPS = 1e-5


def own_wait(eng, spare, s, value):
    eng.wait_ge(s, value)
    eng.sem_inc(spare, 1)


class Chain:

    def __init__(self, eng, sem, base=0):
        self.eng, self.sem, self.base, self.n = eng, sem, base, 0

    def step(self, ins):
        ins.then_inc(self.sem, 1)
        self.n += 1
        return ins

    def wait(self):
        self.eng.wait_ge(self.sem, self.base + self.n)


def emit_consts(nc, consts, named_sem):
    ident, ones_b, neg_tri, rev, not_first, neg_half, rev_i = consts
    made = named_sem("consts_made")
    built = named_sem("consts_built")
    rev_int = named_sem("rev_int")
    with nc.Block() as block:
        @block.gpsimd
        def _(pool):
            ch = Chain(pool, made)
            ch.step(nc.gpsimd.memset(ident[:], 0.0))
            ch.step(nc.gpsimd.memset(neg_tri[:], -1.0))
            ch.step(nc.gpsimd.iota(rev_i[:], pattern=[[-1, rev_i.shape[1]]], base=rev_i.shape[1],
                                   channel_multiplier=0))
            ch.step(nc.gpsimd.memset(ones_b[:], 1.0))
            ch.step(nc.gpsimd.memset(not_first[:], 1.0))
            ch.step(nc.gpsimd.memset(neg_half[:], -0.5))
            ch.wait()
            nc.gpsimd.affine_select(out=ident[:], in_=ident[:], compare_op=ALU.not_equal, fill=1.0, base=0,
                                    pattern=[[-1, P]], channel_multiplier=1).then_inc(built, 1)
            nc.gpsimd.affine_select(out=neg_tri[:], in_=neg_tri[:], compare_op=ALU.is_ge, fill=0.0, base=0,
                                    pattern=[[-1, P]], channel_multiplier=1).then_inc(built, 1)
            nc.gpsimd.memset(not_first[:, :, 0:1], 0.0).then_inc(built, 1)
            nc.gpsimd.tensor_copy(rev[:], rev_i[:]).then_inc(rev_int, 1)
            pool.wait_ge(built, 3)
            pool.wait_ge(rev_int, 1)


def emit_moe(nc, f, T, E, CAP, F, x_src, mix, out_dst, ln_dst, w, scratch, consts, named_sem):
    D = P
    NT = T // P
    CT = 8
    NCH = NT // CT
    KF = F // P
    NS = -(-CAP // P)
    LAST = CAP - (NS - 1) * P
    NSLOT = E * CAP
    SKIP = 40000.0
    GT = 4
    NG = NT // GT
    assert SKIP > NSLOT and NCH % 2 == 0 and E % 2 == 0

    ident, ones_b, neg_tri, rev, not_first, neg_half, _ = consts
    xe_dram, ye_dram = scratch
    x_v = x_src.rearrange("(c t p) d -> c p t d", p=P, t=CT)
    out_v = out_dst.rearrange("(g t p) d -> g p t d", p=P, t=GT)
    ln_v = None if ln_dst is None else ln_dst.rearrange("(g t p) d -> g p t d", p=P, t=GT)

    top = ExitStack()
    with top:
        def sb(name, shape, dt=F32, ctx=top):
            return ctx.enter_context(nc.sbuf_tensor(f"{name}_{f}", shape, dt))

        def sem(name):
            return named_sem(f"{name}_{f}")

        X = sb("X", [P, NT, D])
        gather_idx = sb("gather_idx", [P, NT, 2], U32)
        gate_wt = sb("gate_wt", [P, NT, 2])
        stats = sb("stats", [P, 2, CT, 6])
        mvc = sb("mvc", [P, 2, CT, 2])
        mv = sb("mv", [P, NT, 2])
        rstd = sb("rstd", [P, NT])
        nmr = sb("nmr", [P, NT])
        var_eps = sb("var_eps", [P, NT])
        neg_mean = sb("neg_mean", [P, NT])

        x_loaded = [sem("x_loaded0"), sem("x_loaded1")]
        x_seen = sem("x_seen")
        st_done = sem("st_done")
        ag_done = sem("ag_done")
        mv_done = sem("mv_done")
        spare_d = sem("spare_d")
        spare_p = sem("spare_p")
        spare_s = sem("spare_s")
        pool_ln = sem("pool_ln")
        zeros_ready = sem("zeros_ready")
        xe_zeroed = sem("xe_zeroed")
        r_loaded = [sem("r_loaded0"), sem("r_loaded1")]
        nwb_loaded = sem("nwb_loaded")
        rmv_done = sem("rmv_done")
        pool_rln = sem("pool_rln")
        rn_ready = sem("rn_ready")
        rn_free = sem("rn_free")
        mixed = sem("mixed")

        ZW = NSLOT * D // P // 10
        assert ZW * 10 * P == NSLOT * D
        zeros = sb("zeros", [P, ZW]) if f == 0 else None
        with ExitStack() as c0:
            xe_flat = xe_dram.rearrange("s d -> (s d)").rearrange("(z p w) -> z p w", p=P, w=ZW)
            if mix is not None:
                r_src, nw, nb = mix
                r_v = r_src.rearrange("(c t p) d -> c p t d", p=P, t=CT)
                R = sb("R", [P, NT, D], F32, c0)
                rn = sb("rn", [P, 2, CT, D], F32, c0)
                nw_b = sb("nw_b", [P, D], F32, c0)
                nb_b = sb("nb_b", [P, D], F32, c0)
            with nc.Block() as block:
                @block.sync
                def _(sp):
                    if mix is not None:
                        sp.dma_start(nw_b[:], nw.partition_broadcast(P)).then_inc(nwb_loaded, 16)
                        sp.dma_start(nb_b[:], nb.partition_broadcast(P)).then_inc(nwb_loaded, 16)
                    with sp.Fori(0, NCH // 2) as j:
                        for par in range(2):
                            c = 2 * j + par
                            own_wait(sp, spare_s, x_seen, c + 1)
                            sp.dma_start(X[:, bass.ds(c * CT, CT), :], x_v[c]).then_inc(x_loaded[par], 16)
                            if mix is not None:
                                sp.dma_start(R[:, bass.ds(c * CT, CT), :], r_v[c]).then_inc(r_loaded[par], 16)
                    if f == 0:
                        sp.wait_ge(zeros_ready, 1)
                        for z in range(10):
                            sp.dma_start(xe_flat[z], zeros[:]).then_inc(xe_zeroed, 16)

                @block.vector
                def _(dve):
                    dve.sem_inc(x_seen, 2)

                    def statistics(src, j, par, base):
                        c = 2 * j + par
                        for t in range(CT):
                            ins = nc.vector.bn_stats(stats[:, par, t, :], src[:, bass.ds(c * CT + t, 1), :])
                        ins.then_inc(st_done, 1)
                        own_wait(dve, spare_d, st_done, base + c + 1)
                        for t in range(CT):
                            ins = nc.vector.bn_aggr(mvc[:, par, t, :], stats[:, par, t, :])
                        ins.then_inc(ag_done, 1)
                        dve.wait_ge(ag_done, base + c + 1)
                        return nc.vector.tensor_copy(mv[:, bass.ds(c * CT, CT), :], mvc[:, par])

                    if mix is None:
                        with dve.Fori(0, NCH // 2) as j:
                            for par in range(2):
                                dve.wait_ge(x_loaded[par], 16 * j + 16)
                                statistics(X, j, par, 0).then_inc(mv_done, 1)
                                dve.sem_inc(x_seen, 1)
                                dve.wait_ge(mv_done, 2 * j + par + 1)
                    else:
                        with dve.Fori(0, NCH // 2) as j:
                            for par in range(2):
                                dve.wait_ge(r_loaded[par], 16 * j + 16)
                                dve.wait_ge(x_loaded[par], 16 * j + 16)
                                statistics(R, j, par, 0).then_inc(rmv_done, 1)
                                dve.sem_inc(x_seen, 1)
                                dve.wait_ge(rmv_done, 2 * j + par + 1)
                        dve.wait_ge(nwb_loaded, 32)
                        with dve.Fori(0, NCH // 2) as j:
                            for par in range(2):
                                c = 2 * j + par
                                dve.wait_ge(rn_ready, c + 1)
                                ch = Chain(dve, mixed, 3 * c)
                                rp = rn[:, par]
                                ch.step(nc.vector.tensor_tensor(
                                    rp, rp, nw_b[:].unsqueeze(1).to_broadcast([P, CT, D]), ALU.mult))
                                ch.wait()
                                ch.step(nc.vector.tensor_tensor(
                                    rp, rp, nb_b[:].unsqueeze(1).to_broadcast([P, CT, D]), ALU.add))
                                ch.wait()
                                xc = X[:, bass.ds(c * CT, CT), :]
                                ch.step(nc.vector.tensor_tensor(xc, xc, rp, ALU.add))
                                ch.wait()
                                dve.sem_inc(rn_free, 1)
                                dve.wait_ge(pool_rln, 4)
                                statistics(X, j, par, NCH).then_inc(mv_done, 1)
                                dve.wait_ge(mv_done, c + 1)

                @block.gpsimd
                def _(pool):
                    if f == 0:
                        nc.gpsimd.memset(zeros[:], 0.0).then_inc(zeros_ready, 1)

                    def norm_scalars(s):
                        ch = Chain(pool, s)
                        ch.step(nc.gpsimd.tensor_scalar(var_eps[:], mv[:, :, 1], EPS, None, ALU.add))
                        ch.step(nc.gpsimd.tensor_scalar(neg_mean[:], mv[:, :, 0], -1.0, None, ALU.mult))
                        ch.wait()
                        ch.step(nc.gpsimd.tensor_tensor(rstd[:], var_eps[:], neg_half[:], ALU.pow))
                        ch.wait()
                        ch.step(nc.gpsimd.tensor_tensor(nmr[:], neg_mean[:], rstd[:], ALU.mult))
                        ch.wait()

                    if mix is not None:
                        pool.wait_ge(rmv_done, NCH)
                        norm_scalars(pool_rln)
                        pool.wait_ge(rn_ready, NCH)
                    pool.wait_ge(mv_done, NCH)
                    norm_scalars(pool_ln)

                @block.scalar
                def _(act):
                    if mix is not None:
                        act.sem_inc(rn_free, 2)
                        act.wait_ge(pool_rln, 4)
                        with act.Fori(0, NCH // 2) as j:
                            for par in range(2):
                                c = 2 * j + par
                                act.wait_ge(rn_free, c + 1)
                                for t in range(CT):
                                    k = bass.ds(c * CT + t, 1)
                                    ins = nc.scalar.activation(rn[:, par, t, :], R[:, k, :], ACT.Identity,
                                                               bias=nmr[:, k], scale=rstd[:, k])
                                ins.then_inc(rn_ready, 1)

        xn_ready = sem("xn_ready")
        pt_ready = sem("pt_ready")
        xnT_ready = sem("xnT_ready")
        lg_ready = sem("lg_ready")
        lg_read = sem("lg_read")
        route = sem("route")
        counts_ready = sem("counts_ready")
        pos_ready = sem("pos_ready")
        gap_ready = sem("gap_ready")
        e_ready = sem("e_ready")
        sidx_ready = sem("sidx_ready")
        scattered = [sem("scattered0"), sem("scattered1")]
        gw_loaded = sem("gw_loaded")
        gb_loaded = sem("gb_loaded")
        carry_zero = sem("carry_zero")

        with ExitStack() as c1:
            def sb1(name, shape, dt=F32):
                return sb(name, shape, dt, c1)

            def pb1(name, shape, dt=F32):
                return c1.enter_context(nc.psum_tensor(f"{name}_{f}", shape, dt))

            gate_w = sb1("gate_w", [P, E])
            gate_b = sb1("gate_b", [P, E])
            xn = sb1("xn", [P, 2, CT, D])
            xnT = sb1("xnT", [P, CT * P])
            L = sb1("L", [P, CT, E])
            L2 = sb1("L2", [P, CT, E])
            eq = sb1("eq", [P, 2, CT, E])
            oh = sb1("oh", [P, 2, CT, E])
            chosen = sb1("chosen", [P, E, CT], BF16)
            counts = sb1("counts", [P, E, CT], BF16)
            carry = sb1("carry", [P, E], BF16)
            top_l = sb1("top_l", [P, 2, CT])
            top_r = sb1("top_r", [P, 2, CT])
            pos = sb1("pos", [P, 2, CT])
            first_slot = sb1("first_slot", [P, 2, CT])
            slot = sb1("slot", [P, 2, CT])
            over = sb1("over", [P, 2, CT])
            keep = sb1("keep", [P, 2, CT])
            clip = sb1("clip", [P, 2, CT])
            gap = sb1("gap", [P, CT])
            egap = sb1("egap", [P, CT])
            den = sb1("den", [P, CT])
            share = sb1("share", [P, 2, CT])
            sidx = sb1("sidx", [P, 2, 2, CT], U32)
            PT = pb1("PT", [P, CT * P])
            LG = pb1("LG", [P, CT, E])
            POS = pb1("POS", [P, E, CT])
            ROUTE_STEPS = 28

            with nc.Block() as block:
                @block.sync
                def _(sp):
                    sp.dma_start(gate_w[:], w["gate_w"]).then_inc(gw_loaded, 16)
                    sp.dma_start(gate_b[:], w["gate_b"].partition_broadcast(P)).then_inc(gb_loaded, 16)

                @block.scalar
                def _(act):
                    act.wait_ge(pool_ln, 4)
                    with act.Fori(0, NCH // 2) as j:
                        for par in range(2):
                            c = 2 * j + par
                            act.wait_ge(scattered[par], 256 * j)
                            for t in range(CT):
                                k = bass.ds(c * CT + t, 1)
                                ins = nc.scalar.activation(xn[:, par, t, :], X[:, k, :], ACT.Identity,
                                                           bias=nmr[:, k], scale=rstd[:, k])
                            ins.then_inc(xn_ready, 1)
                            act.wait_ge(pt_ready, c + 1)
                            act.wait_ge(lg_ready, c)
                            nc.scalar.copy(xnT[:], PT[:]).then_inc(xnT_ready, 1)
                            act.wait_ge(gap_ready, c + 1)
                            nc.scalar.activation(egap[:], gap[:], ACT.Exp).then_inc(e_ready, 1)

                @block.tensor
                def _(pe):
                    pe.wait_ge(gw_loaded, 16)
                    with pe.Fori(0, NCH // 2) as j:
                        for par in range(2):
                            c = 2 * j + par
                            pe.wait_ge(xn_ready, c + 1)
                            pe.wait_ge(xnT_ready, c)
                            for t in range(CT):
                                ins = nc.tensor.transpose(PT[:, t * P:(t + 1) * P], xn[:, par, t, :], ident[:])
                            ins.then_inc(pt_ready, 1)
                            pe.wait_ge(xnT_ready, c + 1)
                            pe.wait_ge(lg_read, c)
                            for t in range(CT):
                                ins = nc.tensor.matmul(LG[:, t, :], xnT[:, t * P:(t + 1) * P], gate_w[:],
                                                       start=True, stop=True)
                            ins.then_inc(lg_ready, 1)
                            pe.wait_ge(counts_ready, c + 1)
                            flat = "p e t -> p (e t)"
                            nc.tensor.matmul(POS[:].rearrange(flat), ones_b[:], counts[:].rearrange(flat),
                                             start=True, stop=False)
                            nc.tensor.matmul(POS[:], ones_b[:],
                                             carry[:].unsqueeze(2).to_broadcast([P, E, CT]),
                                             start=False, stop=False)
                            nc.tensor.matmul(POS[:].rearrange(flat), neg_tri[:], chosen[:].rearrange(flat),
                                             start=False, stop=True).then_inc(pos_ready, 1)

                @block.vector
                def _(dve):
                    v = nc.vector
                    ch0 = Chain(dve, carry_zero)
                    ch0.step(v.memset(carry[:], 0.0))
                    ch0.wait()
                    dve.wait_ge(gb_loaded, 16)
                    bce = [P, CT, E]

                    def per_token(a):
                        return a.unsqueeze(2).to_broadcast(bce)

                    rev_b = rev[:].unsqueeze(1).to_broadcast(bce)
                    with dve.Fori(0, NCH // 2) as j:
                        for par in range(2):
                            c = 2 * j + par
                            ch = Chain(dve, route, ROUTE_STEPS * c)
                            dve.wait_ge(lg_ready, c + 1)
                            ch.step(v.tensor_tensor(L[:], LG[:], gate_b[:].unsqueeze(1).to_broadcast(bce), ALU.add))
                            ch.wait()
                            dve.sem_inc(lg_read, 1)
                            for k, src in ((0, L), (1, L2)):
                                ch.step(v.tensor_reduce(top_l[:, k, :], src[:], AX_X, ALU.max))
                                ch.wait()
                                ch.step(v.tensor_tensor(eq[:, k], src[:], per_token(top_l[:, k, :]), ALU.is_equal))
                                ch.wait()
                                ch.step(v.tensor_tensor(eq[:, k], eq[:, k], rev_b, ALU.mult))
                                ch.wait()
                                ch.step(v.tensor_reduce(top_r[:, k, :], eq[:, k], AX_X, ALU.max))
                                ch.wait()
                                ch.step(v.tensor_tensor(oh[:, k], rev_b, per_token(top_r[:, k, :]), ALU.is_equal))
                                ch.wait()
                                if k == 0:
                                    ch.step(v.scalar_tensor_tensor(L2[:], oh[:, 0], -3e38, L[:],
                                                                   ALU.mult, ALU.add))
                                    ch.wait()
                            ch.step(v.tensor_tensor(chosen[:].rearrange("p e t -> p t e"), oh[:, 0], oh[:, 1],
                                                    ALU.add))
                            ch.step(v.tensor_tensor(gap[:], top_l[:, 1, :], top_l[:, 0, :], ALU.subtract))
                            ch.wait()
                            dve.sem_inc(gap_ready, 1)
                            v.tensor_tensor_scan(counts[:].rearrange("p e t -> p (e t)"),
                                                 not_first[:].rearrange("p e t -> p (e t)"),
                                                 chosen[:].rearrange("p e t -> p (e t)"), 0.0,
                                                 ALU.mult, ALU.add).then_inc(counts_ready, 1)
                            ch.step(v.tensor_scalar(first_slot[:], top_r[:], float(-CAP), float(E * CAP),
                                                    ALU.mult, ALU.add))
                            dve.wait_ge(e_ready, c + 1)
                            ch.step(v.tensor_scalar(den[:], egap[:], 1.0, None, ALU.add))
                            ch.wait()
                            ch.step(v.reciprocal(share[:, 0, :], den[:]))
                            ch.wait()
                            ch.step(v.tensor_tensor(share[:, 1, :], share[:, 0, :], egap[:], ALU.mult))
                            dve.wait_ge(pos_ready, c + 1)
                            ch.step(v.tensor_tensor(eq[:, 0], oh[:, 0], POS[:].rearrange("p e t -> p t e"),
                                                    ALU.mult))
                            ch.step(v.tensor_tensor(eq[:, 1], oh[:, 1], POS[:].rearrange("p e t -> p t e"),
                                                    ALU.mult))
                            ch.step(v.tensor_tensor(carry[:], carry[:], counts[:, :, CT - 1], ALU.add))
                            ch.wait()
                            ch.step(v.tensor_reduce(pos[:], eq[:], AX_X, ALU.add))
                            ch.wait()
                            ch.step(v.tensor_tensor(slot[:], first_slot[:], pos[:], ALU.add))
                            ch.step(v.tensor_scalar(over[:], pos[:], float(CAP), None, ALU.is_ge))
                            ch.step(v.tensor_scalar(keep[:], pos[:], float(CAP), 0.5, ALU.is_lt, ALU.mult))
                            ch.step(v.tensor_scalar(clip[:], pos[:], float(CAP - 1), None, ALU.min))
                            ch.wait()
                            dve.wait_ge(scattered[par], 256 * j)
                            v.scalar_tensor_tensor(sidx[:, par], over[:], SKIP, slot[:],
                                                   ALU.mult, ALU.add).then_inc(sidx_ready, 1)
                            tiles = bass.ds(c * CT, CT)
                            ch.step(v.tensor_tensor(gather_idx[:, tiles, :].rearrange("p t k -> p k t"),
                                                    first_slot[:], clip[:], ALU.add))
                            ch.step(v.tensor_tensor(gate_wt[:, tiles, :].rearrange("p t k -> p k t"),
                                                    share[:], keep[:], ALU.mult))
                            assert ch.n == ROUTE_STEPS, ch.n
                            ch.wait()

                @block.gpsimd
                def _(pool):
                    if f == 0:
                        pool.wait_ge(xe_zeroed, 160)
                    with pool.Fori(0, NCH // 2) as j:
                        for par in range(2):
                            own_wait(pool, spare_p, sidx_ready, 2 * j + par + 1)
                            for t in range(CT):
                                for k in range(2):
                                    nc.gpsimd.indirect_dma_start(
                                        out=xe_dram, in_=xn[:, par, t, :], in_offset=None,
                                        out_offset=bass.IndirectOffsetOnAxis(ap=sidx[:, par, k, t:t + 1], axis=0),
                                        bounds_check=NSLOT - 1, oob_is_err=False).then_inc(scattered[par], 16)
                    for par in range(2):
                        pool.wait_ge(scattered[par], 256 * (NCH // 2))

        w1_loaded = [sem("w1_loaded0"), sem("w1_loaded1")]
        w2_loaded = [sem("w2_loaded0"), sem("w2_loaded1")]
        xe_loaded = [sem("xe_loaded0"), sem("xe_loaded1")]
        xt_ready = sem("xt_ready")
        xt_copied = sem("xt_copied")
        h_ready = sem("h_ready")
        g_ready = sem("g_ready")
        y_ready = sem("y_ready")
        y_copied = sem("y_copied")
        ye_stored = [sem("ye_stored0"), sem("ye_stored1")]
        b1_loaded = sem("b1_loaded")
        b2_loaded = sem("b2_loaded")

        with ExitStack() as c2:
            def sb2(name, shape, dt=F32):
                return sb(name, shape, dt, c2)

            def pb2(name, shape, dt=F32):
                return c2.enter_context(nc.psum_tensor(f"{name}_{f}", shape, dt))

            w1 = sb2("w1", [P, 2, F])
            w2 = sb2("w2", [P, 2, KF, D])
            xe = sb2("xe", [P, 2, NS, D])
            xeT = sb2("xeT", [P, 2, NS * P])
            hT = sb2("hT", [P, 2, KF, CAP])
            ye = sb2("ye", [P, 2, NS, D])
            b1 = sb2("b1", [P, E * KF])
            b2 = sb2("b2", [P, E, D])
            XT = pb2("XT", [P, 1024])
            H = pb2("H", [P, 2, 1024])
            Y = pb2("Y", [P, 1024])
            SLOTS = [(s * P, P if s < NS - 1 else LAST) for s in range(NS)]
            FULL = (NS - 1) * P

            with nc.Block() as block:
                @block.sync
                def _(sp):
                    sp.dma_start(b1[:], w["b1"]).then_inc(b1_loaded, 16)
                    sp.dma_start(b2[:], w["b2"].partition_broadcast(P)).then_inc(b2_loaded, 16)
                    with sp.Fori(0, E // 2) as j:
                        for par in range(2):
                            e = 2 * j + par
                            own_wait(sp, spare_s, xt_ready, e + 1)
                            rows = xe_dram[bass.ds(e * CAP, CAP), :]
                            sp.dma_start(xe[:, par, 0:NS - 1, :],
                                         rows[0:FULL, :].rearrange("(s p) d -> p s d", p=P)
                                         ).then_inc(xe_loaded[par], 16)
                            sp.dma_start(xe[0:LAST, par, NS - 1, :], rows[FULL:CAP, :]
                                         ).then_inc(xe_loaded[par], 16)
                            own_wait(sp, spare_s, h_ready, KF * e + KF)
                            sp.dma_start(w1[:, par, :], w["w1"][e]).then_inc(w1_loaded[par], 16)
                            own_wait(sp, spare_s, y_ready, e + 1)
                            sp.dma_start(w2[:, par], w["w2"][e].rearrange("(k p) d -> p k d", p=P)
                                         ).then_inc(w2_loaded[par], 16)

                @block.tensor
                def _(pe):
                    pe.sem_inc(xt_ready, 2)
                    pe.sem_inc(h_ready, 2 * KF)
                    pe.sem_inc(y_ready, 2)
                    with pe.Fori(0, E // 2) as j:
                        for par in range(2):
                            e = 2 * j + par
                            pe.wait_ge(xe_loaded[par], 32 * j + 32)
                            pe.wait_ge(xt_copied, e)
                            for s, (at, n) in enumerate(SLOTS):
                                ins = nc.tensor.transpose(XT[:, at:at + n], xe[0:n, par, s, :], ident[0:n, 0:n])
                            ins.then_inc(xt_ready, 1)
                            pe.wait_ge(xt_copied, e + 1)
                            pe.wait_ge(w1_loaded[par], 16 * j + 16)
                            for k in range(KF):
                                pe.wait_ge(g_ready, KF * e + k + 1)
                                for a, b in ((0, 512), (512, CAP)):
                                    ins = nc.tensor.matmul(H[:, k % 2, a:b], w1[:, par, k * P:(k + 1) * P],
                                                           xeT[:, par, a:b], start=True, stop=True)
                                ins.then_inc(h_ready, 1)
                            pe.wait_ge(g_ready, 2 + KF * e + KF)
                            pe.wait_ge(w2_loaded[par], 16 * j + 16)
                            pe.wait_ge(y_copied, e)
                            for s, (at, n) in enumerate(SLOTS):
                                for k in range(KF):
                                    ins = nc.tensor.matmul(Y[0:n, s * D:(s + 1) * D], hT[:, par, k, at:at + n],
                                                           w2[:, par, k, :], start=(k == 0), stop=(k == KF - 1))
                            ins.then_inc(y_ready, 1)

                @block.scalar
                def _(act):
                    act.sem_inc(g_ready, 2)
                    act.wait_ge(b1_loaded, 16)
                    with act.Fori(0, E // 2) as j:
                        for par in range(2):
                            e = 2 * j + par
                            act.wait_ge(y_ready, e + 1)
                            for k in range(KF):
                                act.wait_ge(h_ready, 2 * KF + KF * e + k + 1)
                                nc.scalar.activation(hT[:, par, k, :], H[:, k % 2, 0:CAP], ACT.Gelu,
                                                     bias=b1[:, bass.ds(e * KF + k, 1)]).then_inc(g_ready, 1)

                @block.vector
                def _(dve):
                    dve.wait_ge(b2_loaded, 16)
                    with dve.Fori(0, E // 2) as j:
                        for par in range(2):
                            e = 2 * j + par
                            dve.wait_ge(xt_ready, e + 3)
                            dve.wait_ge(h_ready, KF * e + KF)
                            nc.vector.tensor_copy(xeT[:, par, 0:CAP], XT[:, 0:CAP]).then_inc(xt_copied, 1)
                            dve.wait_ge(y_ready, e + 3)
                            dve.wait_ge(ye_stored[par], 32 * j)
                            bias = b2[:, bass.ds(e, 1), :]
                            nc.vector.tensor_tensor(
                                ye[:, par, 0:NS - 1, :], Y[:, 0:FULL].rearrange("p (s d) -> p s d", d=D),
                                bias.to_broadcast([P, NS - 1, D]), ALU.add)
                            nc.vector.tensor_tensor(
                                ye[0:LAST, par, NS - 1:NS, :],
                                Y[0:LAST, FULL:FULL + D].rearrange("p (s d) -> p s d", d=D),
                                bias[0:LAST], ALU.add).then_inc(y_copied, 1)

                @block.gpsimd
                def _(pool):
                    with pool.Fori(0, E // 2) as j:
                        for par in range(2):
                            e = 2 * j + par
                            pool.wait_ge(y_copied, e + 1)
                            rows = ye_dram[bass.ds(e * CAP, CAP), :]
                            pool.dma_start(rows[0:FULL, :].rearrange("(s p) d -> p s d", p=P),
                                           ye[:, par, 0:NS - 1, :]).then_inc(ye_stored[par], 16)
                            pool.dma_start(rows[FULL:CAP, :], ye[0:LAST, par, NS - 1, :]
                                           ).then_inc(ye_stored[par], 16)
                    for par in range(2):
                        pool.wait_ge(ye_stored[par], 32 * (E // 2))

        idx_ready = sem("idx_ready")
        gathered = [sem("gathered0"), sem("gathered1")]
        summed = sem("summed")
        out_stored = [sem("out_stored0"), sem("out_stored1")]
        cst = sem("cst")
        cmv = sem("cmv")
        crs = sem("crs")
        ln_ready = sem("ln_ready")
        ln_stored = [sem("ln_stored0"), sem("ln_stored1")]

        with ExitStack() as c3:
            def sb3(name, shape, dt=F32):
                return sb(name, shape, dt, c3)

            part = sb3("part", [P, 2, 2, GT, D])
            idx = sb3("idx", [P, 2, 2, GT], U32)
            xo = sb3("xo", [P, 2, GT, D])
            cstat = sb3("cstat", [P, 2, GT, 6])
            cmvt = sb3("cmvt", [P, 2, GT, 2])
            cve = sb3("cve", [P, 2, GT])
            cnm = sb3("cnm", [P, 2, GT])
            crstd = sb3("crstd", [P, 2, GT])
            cnmr = sb3("cnmr", [P, 2, GT])
            xln = sb3("xln", [P, 2, GT, D])

            with nc.Block() as block:
                @block.gpsimd
                def _(pool):
                    def norm_scalars(g, par):
                        own_wait(pool, spare_p, cmv, g + 1)
                        own_wait(pool, spare_p, ln_ready, g + 1)
                        ch = Chain(pool, crs, 8 + 4 * g)
                        ch.step(nc.gpsimd.tensor_scalar(cve[:, par], cmvt[:, par, :, 1], EPS, None, ALU.add))
                        ch.step(nc.gpsimd.tensor_scalar(cnm[:, par], cmvt[:, par, :, 0], -1.0, None, ALU.mult))
                        ch.wait()
                        ch.step(nc.gpsimd.tensor_tensor(crstd[:, par], cve[:, par], neg_half[:, 0:GT], ALU.pow))
                        ch.wait()
                        ch.step(nc.gpsimd.tensor_tensor(cnmr[:, par], cnm[:, par], crstd[:, par], ALU.mult))
                        ch.wait()

                    def gathers(j, par):
                        g = 2 * j + par
                        own_wait(pool, spare_p, gathered[par], 16 * 2 * GT * j)
                        nc.gpsimd.tensor_copy(
                            idx[:, par], gather_idx[:, bass.ds(g * GT, GT), :].rearrange("p t k -> p k t")
                        ).then_inc(idx_ready, 1)
                        own_wait(pool, spare_p, idx_ready, g + 1)
                        own_wait(pool, spare_p, summed, 2 * g + 2)
                        for t in range(GT):
                            for k in range(2):
                                nc.gpsimd.indirect_dma_start(
                                    out=part[:, par, k, t, :], out_offset=None, in_=ye_dram,
                                    in_offset=bass.IndirectOffsetOnAxis(ap=idx[:, par, k, t:t + 1], axis=0)
                                ).then_inc(gathered[par], 16)

                    pool.sem_inc(crs, 8)
                    gathers(0, 0)
                    gathers(0, 1)
                    with pool.Fori(1, NG // 2) as j:
                        for par in range(2):
                            gathers(j, par)
                            if ln_dst is not None:
                                norm_scalars(2 * j + par - 2, par)
                    if ln_dst is not None:
                        norm_scalars(NG - 2, 0)
                        norm_scalars(NG - 1, 1)

                @block.vector
                def _(dve):
                    dve.sem_inc(summed, 4)
                    with dve.Fori(0, NG // 2) as j:
                        for par in range(2):
                            g = 2 * j + par
                            dve.wait_ge(gathered[par], 16 * 2 * GT * (j + 1))
                            dve.wait_ge(out_stored[par], 16 * j)
                            if ln_dst is not None:
                                dve.wait_ge(ln_ready, g + 1)
                            ch = Chain(dve, summed, 4 + 2 * g)
                            for k in range(2):
                                for t in range(GT):
                                    tile = bass.ds(g * GT + t, 1)
                                    src = X[:, tile, :] if k == 0 else xo[:, par, t:t + 1, :]
                                    ins = nc.vector.scalar_tensor_tensor(
                                        xo[:, par, t:t + 1, :], part[:, par, k, t:t + 1, :],
                                        gate_wt[:, tile, k], src, ALU.mult, ALU.add)
                                ch.step(ins)
                                ch.wait()
                            if ln_dst is not None:
                                dve.wait_ge(crs, 4 * g + 4)
                                for t in range(GT):
                                    ins = nc.vector.bn_stats(cstat[:, par, t, :], xo[:, par, t, :])
                                ins.then_inc(cst, 1)
                                own_wait(dve, spare_d, cst, g + 1)
                                for t in range(GT):
                                    ins = nc.vector.bn_aggr(cmvt[:, par, t, :], cstat[:, par, t, :])
                                ins.then_inc(cmv, 1)

                @block.scalar
                def _(act):
                    if ln_dst is not None:
                        act.sem_inc(ln_ready, 2)
                        with act.Fori(0, NG // 2) as j:
                            for par in range(2):
                                g = 2 * j + par
                                act.wait_ge(crs, 8 + 4 * g + 4)
                                act.wait_ge(ln_stored[par], 16 * j)
                                for t in range(GT):
                                    ins = nc.scalar.activation(xln[:, par, t, :], xo[:, par, t, :], ACT.Identity,
                                                               bias=cnmr[:, par, t:t + 1],
                                                               scale=crstd[:, par, t:t + 1])
                                ins.then_inc(ln_ready, 1)

                @block.sync
                def _(sp):
                    with sp.Fori(0, NG // 2) as j:
                        for par in range(2):
                            g = 2 * j + par
                            own_wait(sp, spare_s, summed, 4 + 2 * g + 2)
                            if ln_dst is not None:
                                own_wait(sp, spare_s, ln_ready, g + 3)
                                sp.dma_start(ln_v[g], xln[:, par]).then_inc(ln_stored[par], 16)
                            sp.dma_start(out_v[g], xo[:, par]).then_inc(out_stored[par], 16)
                    for par in range(2):
                        sp.wait_ge(out_stored[par], 16 * (NG // 2))
                        if ln_dst is not None:
                            own_wait(sp, spare_s, ln_stored[par], 16 * (NG // 2))


def emit_attention(nc, T, D, io, r_dram, consts, named_sem):
    ident, neg_half = consts[0], consts[5]
    L = 512
    NL = io["wpack"].shape[0]
    U = 2 * L
    CT = U // P
    NPAIR = T // U
    NU = NL * NPAIR
    EH = 2
    DI = EH * P
    DC = 4
    NST = 16
    RK = D // 16
    NX = RK + 2 * NST
    RING = 4
    HEADS = 16
    MAKE_AT = {0: (4,), 2: (5,), 3: (6, 7), 4: (8,), 5: (9,), 8: (10, 11), 9: (12, 13, 14, 15)}
    EVICT_AT = {1: (0, 1), 5: (2, 3), 6: (4,), 7: (5,), 8: (6, 7), 9: (8,), 10: (9,), 12: (10, 11),
                13: (12, 13, 14, 15)}
    OZ = 0
    OTAP = OZ + DI
    OXP = OTAP + DC * DI
    ODT = OXP + EH * NX
    OLW = ODT + DI
    OLB = OLW + 1
    OCB = OLB + 1
    ODB = OCB + EH
    NW = ODB + EH
    OOW = 0
    OA = OOW + EH * D
    OD = OA + EH * NST
    NLATE = OD + EH

    pack_dram = nc.dram_tensor("head_pack", (NL, P, NW), F32).ap()
    late_dram = nc.dram_tensor("late_pack", (NL, P, NLATE), F32).ap()
    bc_dram = nc.dram_tensor("bc_rows", (2, 2 * NST, U), F32).ap()

    top = ExitStack()
    with top:
        def sb(name, shape, dt=F32, ctx=top):
            return ctx.enter_context(nc.sbuf_tensor(name, shape, dt))

        def sem(name):
            return named_sem(name)

        raw_loaded = sem("raw_loaded")
        a_exp = sem("a_exp")
        folded = sem("folded")
        pack_stored = sem("pack_stored")
        with ExitStack() as c0:
            pk = sb("pk", [P, NL, NW], F32, c0)
            lt = sb("lt", [P, NL, NLATE], F32, c0)
            in_x = sb("in_x_sb", [P, NL, DI], F32, c0)
            taps = sb("taps", [P, NL, DC, DI], F32, c0)
            with nc.Block() as block:
                @block.sync
                def _(sp):
                    for l in range(NL):
                        sp.dma_start(pk[:, l, OZ:OTAP], io["wpack"][l, :, 0:DI]).then_inc(raw_loaded, 16)
                        sp.dma_start(pk[:, l, OXP:NW], io["wpack"][l, :, DI:]).then_inc(raw_loaded, 16)
                        sp.dma_start(lt[:, l, :], io["late"][l]).then_inc(raw_loaded, 16)
                        sp.dma_start(in_x[:, l, :], io["in_x"][l]).then_inc(raw_loaded, 16)
                        sp.dma_start(taps[:, l], io["conv_w"][l].partition_broadcast(P)).then_inc(raw_loaded, 16)
                    sp.wait_ge(folded, 2 * NL)
                    for l in range(NL):
                        sp.dma_start(pack_dram[l], pk[:, l, :]).then_inc(pack_stored, 16)
                        sp.dma_start(late_dram[l], lt[:, l, :]).then_inc(pack_stored, 16)
                    sp.wait_ge(pack_stored, 32 * NL)

                @block.scalar
                def _(act):
                    act.wait_ge(raw_loaded, 80 * NL)
                    nc.scalar.activation(lt[:, :, OA:OD], lt[:, :, OA:OD], ACT.Exp).then_inc(a_exp, 1)

                @block.vector
                def _(dve):
                    dve.wait_ge(raw_loaded, 80 * NL)
                    for l in range(NL):
                        nc.vector.tensor_tensor(
                            pk[:, l, OTAP:OXP].rearrange("p (k e) -> p k e", k=DC), taps[:, l],
                            in_x[:, l, :].unsqueeze(1).to_broadcast([P, DC, DI]), ALU.mult).then_inc(folded, 1)
                    dve.wait_ge(a_exp, 1)
                    for l in range(NL):
                        nc.vector.tensor_scalar(lt[:, l, OA:OD], lt[:, l, OA:OD], -1.0, None,
                                                ALU.mult).then_inc(folded, 1)

        W = sb("W", [P, NW])
        late = sb("late", [P, 2, NLATE])
        r_head = sb("r_head", [P, CT, D])
        r_tail = sb("r_tail", [P, CT, D])
        hstat = sb("hstat", [P, CT, 6])
        hmv = sb("hmv", [P, CT, 2])
        h_ve = sb("h_ve", [P, CT])
        h_nm = sb("h_nm", [P, CT])
        h_rstd = sb("h_rstd", [P, CT])
        h_nmr = sb("h_nmr", [P, CT])
        xn = sb("xn_a", [P, CT, D])
        hT = sb("hT_a", [P, 2, DC - 1 + L])
        xc = sb("xc", [P, 2, EH, U])
        zs = sb("zs", [P, 2, EH, U])
        dt = sb("dt", [P, 2, EH, U])
        dtx = sb("dtx", [P, 2, EH, U])
        dblT = sb("dblT", [NX, U])
        yb = sb("yb", [P, EH, U])
        ln_u = sb("ln_u", [P, EH, U])
        dA = sb("dA", [P, 2, EH, 2, L])
        H = sb("Hst", [P, RING, EH, U])
        Bb = sb("Bb", [P, RING, U])
        Cb = sb("Cb", [P, RING, U])
        Y = top.enter_context(nc.psum_tensor("Y_a", [P, EH, U], F32))
        HB = top.enter_context(nc.psum_tensor("HB_a", [P, 2, 512], F32))
        OUT = top.enter_context(nc.psum_tensor("OUT_a", [P, CT, D], F32))

        w_loaded = sem("w_loaded")
        late_loaded = sem("late_loaded")
        rh_loaded = sem("rh_loaded")
        rt_loaded = sem("rt_loaded")
        r_stored = sem("r_stored")
        B_loaded = [sem(f"B_loaded{i}") for i in range(RING)]
        C_loaded = [sem(f"C_loaded{i}") for i in range(RING)]
        bc_stored = sem("bc_stored")
        hst_done = sem("hst_done")
        hmv_ready = sem("hmv_ready")
        hscal = sem("hscal")
        xn_done = sem("xn_done")
        hb_full = sem("hb_full")
        hb_free = sem("hb_free")
        silu_done = sem("silu_done")
        exp_done = sem("exp_done")
        ln_done = sem("ln_done")
        one_u = sem("one_u")
        ln_exact = sem("ln_exact")
        lost_ready = sem("lost_ready")
        dt_half = sem("dt_half")
        dt_ready = sem("dt_ready")
        dtx_ready = sem("dtx_ready")
        dA_ready = sem("dA_ready")
        dbu = sem("dbu")
        scanned = sem("scanned")
        g_made = sem("g_made")
        reduced = sem("reduced")
        y_read = sem("y_read")
        yb_ready = sem("yb_ready")
        out_ready = sem("out_ready")
        r_ready = sem("r_ready")
        zero_pads = sem("zero_pads")
        spare_d = sem("spare_d")
        spare_p = sem("spare_p")
        spare_s = sem("spare_s")

        r_units = r_dram.rearrange("l (u t p) d -> (l u) p t d", p=P, t=CT)

        def more(u):
            return not isinstance(u, int) or u + 2 < NU

        def units(fori, head0, body, tail_last):
            head0()
            body(0, 0, False, True)
            body(1, 1, True, True)
            with fori(1, NU // 2 - 1) as j:
                for par in range(2):
                    body(2 * j + par, par, True, True)
            body(NU - 2, 0, True, True)
            body(NU - 1, 1, True, False)
            tail_last()

        with nc.Block() as block:
            @block.sync
            def _(sp):
                def load_weights(v):
                    sp.wait_ge(hb_free, HEADS * v + 2)
                    sp.dma_start(W[:], pack_dram[v // NPAIR]).then_inc(w_loaded, 16)

                def load_late(v, q):
                    sp.dma_start(late[:, q, :], late_dram[v // NPAIR]).then_inc(late_loaded, 16)

                def load_head_residual(v):
                    own_wait(sp, spare_s, xn_done, v)
                    own_wait(sp, spare_s, r_stored, 16 * v + 16)
                    sp.dma_start(r_head[:], r_units[v]).then_inc(rh_loaded, 16)

                def store_residual(v):
                    own_wait(sp, spare_s, r_ready, v + 1)
                    sp.dma_start(r_units[v + NPAIR], r_tail[:]).then_inc(r_stored, 16)

                def head0():
                    sp.sem_inc(r_stored, 16 * NPAIR)
                    load_weights(0)
                    load_late(0, 0)
                    load_head_residual(0)
                    load_head_residual(1)
                    load_weights(1)

                def body(u, par, tail, head):
                    own_wait(sp, spare_s, bc_stored, 16 * u + 16)
                    for n in range(NST):
                        s = n % RING
                        sp.wait_ge(dbu, NST * u + n + 1)
                        sp.dma_start(Bb[:, s, :], bc_dram[par, n].partition_broadcast(P)).then_inc(B_loaded[s], 16)
                        sp.wait_ge(g_made, NST * u + n + 1)
                        sp.dma_start(Cb[:, s, :], bc_dram[par, NST + n].partition_broadcast(P)
                                     ).then_inc(C_loaded[s], 16)
                        if n == 4 and more(u):
                            load_head_residual(u + 2)
                        if n == 10 and tail:
                            store_residual(u - 1)
                        if n == 11 and head:
                            if tail:
                                own_wait(sp, spare_s, out_ready, u)
                            load_late(u + 1, 1 - par)
                        if n == 12:
                            own_wait(sp, spare_s, r_stored, 16 * NPAIR + 16 * u)
                            sp.dma_start(r_tail[:], r_units[u]).then_inc(rt_loaded, 16)
                    if more(u):
                        load_weights(u + 2)

                def tail_last():
                    store_residual(NU - 1)
                    sp.wait_ge(r_stored, 16 * (NPAIR + NU))

                units(sp.Fori, head0, body, tail_last)

            @block.scalar
            def _(act):
                def normalise(v):
                    act.wait_ge(hscal, 4 * v + 4)
                    act.wait_ge(rh_loaded, 16 * v + 16)
                    for t in range(CT):
                        ins = nc.scalar.activation(xn[:, t, :], r_head[:, t, :], ACT.Identity,
                                                   bias=h_nmr[:, t:t + 1], scale=h_rstd[:, t:t + 1])
                    ins.then_inc(xn_done, 1)

                def evict(v, q, k):
                    ps = HB[:, k % 2, :]
                    act.wait_ge(hb_full, HEADS * v + k + 1)
                    if k < 2:
                        ins = nc.scalar.activation(hT[:, k, DC - 1:], ps, ACT.Identity,
                                                   bias=W[:, OLB:OLB + 1], scale=W[:, OLW:OLW + 1])
                    elif k < 10:
                        b, what = (k - 2) // 4, (k - 2) % 4
                        dst = (zs, xc)[what // 2][:, q, what % 2, b * L:(b + 1) * L]
                        ins = nc.scalar.copy(dst, ps)
                    elif k < 12:
                        ins = nc.scalar.copy(dblT[:, (k - 10) * L:(k - 9) * L], ps[0:NX])
                    else:
                        b, h = (k - 12) // 2, (k - 12) % 2
                        bias = W[:, ODB + h:ODB + h + 1]
                        cols = slice(b * L, (b + 1) * L)
                        nc.scalar.activation(dt[:, q, h, cols], ps, ACT.Relu, bias=bias)
                        ins = nc.scalar.activation(dtx[:, q, h, cols], ps, ACT.Abs, bias=bias)
                    ins.then_inc(hb_free, 1)

                def silus(v, q):
                    act.wait_ge(hb_free, 2 + HEADS * v + 10)
                    for h in range(EH):
                        nc.scalar.activation(xc[:, q, h, :], xc[:, q, h, :], ACT.Silu,
                                             bias=W[:, OCB + h:OCB + h + 1])
                    nc.scalar.activation(zs[:, q], zs[:, q], ACT.Silu).then_inc(silu_done, 1)

                def store_bc(v, q):
                    act.wait_ge(hb_free, 2 + HEADS * v + 12)
                    act.dma_start(bc_dram[q], dblT[RK:NX, :]).then_inc(bc_stored, 16)

                def log_part(v, q):
                    act.wait_ge(hb_free, 2 + HEADS * v + HEADS)
                    nc.scalar.activation(dtx[:, q], dtx[:, q], ACT.Exp, scale=-1.0).then_inc(exp_done, 1)
                    act.wait_ge(exp_done, v + 1)
                    act.wait_ge(dt_ready, v)
                    nc.scalar.activation(ln_u[:], dtx[:, q], ACT.Ln, bias=1.0).then_inc(ln_done, 1)

                def head_piece(n, v, q, tail):
                    if n == 0:
                        normalise(v)
                    if n == 1:
                        act.wait_ge(w_loaded, 16 * v + 16)
                    if n == 5 and tail:
                        act.wait_ge(yb_ready, v - 1)
                    for k in EVICT_AT.get(n, ()):
                        if k == 10:
                            act.wait_ge(bc_stored, 16 * v)
                        evict(v, q, k)
                    if n == 11:
                        silus(v, q)
                    if n == 12:
                        store_bc(v, q)
                    if n == 14:
                        log_part(v, q)

                def head0():
                    act.sem_inc(hb_free, 2)
                    act.wait_ge(zero_pads, 2)
                    for n in range(NST):
                        head_piece(n, 0, 0, False)

                def body(u, par, tail, head):
                    act.wait_ge(dt_ready, u + 1)
                    act.wait_ge(late_loaded, 16 * u + 16)
                    for n in range(NST):
                        act.wait_ge(scanned, NST * u + n + 1)
                        for h in range(EH):
                            a = OA + h * NST + n
                            ins = nc.scalar.activation(
                                dA[:, n % 2, h, :, 1:], dt[:, par, h, :].rearrange("p (b t) -> p b t", b=2)[:, :, 1:],
                                ACT.Exp, scale=late[:, par, a:a + 1])
                        ins.then_inc(dA_ready, 1)
                        if head:
                            head_piece(n, u + 1, 1 - par, tail)

                units(act.Fori, head0, body, lambda: None)

            @block.vector
            def _(dve):
                v_ = nc.vector

                def statistics(v):
                    dve.wait_ge(rh_loaded, 16 * v + 16)
                    for t in range(CT):
                        ins = v_.bn_stats(hstat[:, t, :], r_head[:, t, :])
                    ins.then_inc(hst_done, 1)
                    own_wait(dve, spare_d, hst_done, v + 1)
                    own_wait(dve, spare_d, hscal, 4 * v)
                    for t in range(CT):
                        ins = v_.bn_aggr(hmv[:, t, :], hstat[:, t, :])
                    ins.then_inc(hmv_ready, 1)

                def head_piece(n, v, q, tail):
                    if n == 13:
                        dve.wait_ge(exp_done, v + 1)
                        if tail:
                            dve.wait_ge(out_ready, v - 1)
                        v_.tensor_scalar(yb[:], dtx[:, q], 1.0, -1.0, ALU.add, ALU.add).then_inc(one_u, 1)
                        dve.wait_ge(ln_done, v + 1)
                        own_wait(dve, spare_d, one_u, v + 1)
                        v_.scalar_tensor_tensor(ln_u[:], yb[:], 0.0, ln_u[:], ALU.is_gt, ALU.mult
                                                ).then_inc(ln_exact, 1)
                        dve.wait_ge(ln_exact, v + 1)
                        v_.tensor_tensor(dt[:, q], dt[:, q], ln_u[:], ALU.add).then_inc(dt_half, 1)
                    if n == 14:
                        dve.wait_ge(lost_ready, v + 1)
                        dve.wait_ge(dt_half, v + 1)
                        v_.tensor_tensor(dt[:, q], dt[:, q], yb[:], ALU.add).then_inc(dt_ready, 1)
                    if n == 15:
                        dve.wait_ge(dt_ready, v + 1)
                        v_.tensor_tensor(dtx[:, q], dt[:, q], xc[:, q], ALU.mult).then_inc(dtx_ready, 1)

                def gate(v, q):
                    dve.wait_ge(reduced, RING + NST * v + NST)
                    own_wait(dve, spare_d, out_ready, v)
                    for h in range(EH):
                        ins = v_.scalar_tensor_tensor(yb[:, h, :], xc[:, q, h, :], late[:, q, OD + h:OD + h + 1],
                                                      Y[:, h, :], ALU.mult, ALU.add)
                    ins.then_inc(y_read, 1)
                    dve.wait_ge(y_read, v + 1)
                    v_.tensor_tensor(yb[:], yb[:], zs[:, q], ALU.mult).then_inc(yb_ready, 1)

                def add_residual(v):
                    dve.wait_ge(out_ready, v + 1)
                    dve.wait_ge(rt_loaded, 16 * v + 16)
                    v_.tensor_tensor(r_tail[:], r_tail[:], OUT[:], ALU.add).then_inc(r_ready, 1)

                def head0():
                    dve.sem_inc(dbu, RING)
                    dve.sem_inc(scanned, 2)
                    v_.memset(hT[:, :, 0:DC - 1], 0.0).then_inc(zero_pads, 1)
                    v_.memset(dA[:, :, :, :, 0:1], 0.0).then_inc(zero_pads, 1)
                    statistics(0)
                    for n in range(NST):
                        head_piece(n, 0, 0, False)
                    statistics(1)

                def body(u, par, tail, head):
                    own_wait(dve, spare_d, dtx_ready, u + 1)
                    for n in range(NST):
                        s = n % RING
                        dve.wait_ge(B_loaded[s], 16 * (NST // RING) * u + 16 * (n // RING) + 16)
                        dve.wait_ge(reduced, NST * u + n + 1)
                        v_.tensor_tensor(H[:, s], dtx[:, par], Bb[:, s, :].unsqueeze(1).to_broadcast([P, EH, U]),
                                         ALU.mult).then_inc(dbu, 1)
                        dve.wait_ge(dbu, RING + NST * u + n + 1)
                        dve.wait_ge(dA_ready, NST * u + n + 1)
                        flat = H[:, s].rearrange("p h t -> p (h t)")
                        v_.tensor_tensor_scan(flat, dA[:, n % 2].rearrange("p h b t -> p (h b t)"), flat, 0.0,
                                              ALU.mult, ALU.add).then_inc(scanned, 1)
                        if n == 2 and tail:
                            gate(u - 1, 1 - par)
                        if n == 5 and tail:
                            add_residual(u - 1)
                        if head:
                            head_piece(n, u + 1, 1 - par, tail)
                        if n == 11 and more(u):
                            statistics(u + 2)

                def tail_last():
                    gate(NU - 1, 1)
                    add_residual(NU - 1)

                units(dve.Fori, head0, body, tail_last)

            @block.gpsimd
            def _(pool):
                g_ = nc.gpsimd

                def norm_scalars(v):
                    own_wait(pool, spare_p, hmv_ready, v + 1)
                    own_wait(pool, spare_p, xn_done, v)
                    ch = Chain(pool, hscal, 4 * v)
                    ch.step(g_.tensor_scalar(h_ve[:], hmv[:, :, 1], EPS, None, ALU.add))
                    ch.step(g_.tensor_scalar(h_nm[:], hmv[:, :, 0], -1.0, None, ALU.mult))
                    ch.wait()
                    ch.step(g_.tensor_tensor(h_rstd[:], h_ve[:], neg_half[:, 0:CT], ALU.pow))
                    ch.wait()
                    ch.step(g_.tensor_tensor(h_nmr[:], h_nm[:], h_rstd[:], ALU.mult))

                def lost(v, q):
                    pool.wait_ge(ln_exact, v + 1)
                    g_.tensor_tensor(yb[:], dtx[:, q], yb[:], ALU.subtract).then_inc(lost_ready, 1)

                def head0():
                    pool.sem_inc(g_made, RING)
                    norm_scalars(0)
                    lost(0, 0)
                    norm_scalars(1)

                def body(u, par, tail, head):
                    for n in range(NST):
                        s = n % RING
                        pool.wait_ge(C_loaded[s], 16 * (NST // RING) * u + 16 * (n // RING) + 16)
                        pool.wait_ge(scanned, 2 + NST * u + n + 1)
                        g_.tensor_tensor(H[:, s], H[:, s], Cb[:, s, :].unsqueeze(1).to_broadcast([P, EH, U]),
                                         ALU.mult).then_inc(g_made, 1)
                        if n == 12 and more(u):
                            norm_scalars(u + 2)
                        if n == 12 and head:
                            lost(u + 1, 1 - par)

                units(pool.Fori, head0, body, lambda: None)

            @block.tensor
            def _(pe):
                mm = nc.tensor.matmul

                def product(v, q, k):
                    pe.wait_ge(hb_free, HEADS * v + k + 1)
                    ps = HB[:, k % 2, :]
                    if k < 2:
                        for t in range(4):
                            ins = nc.tensor.transpose(ps[:, t * P:(t + 1) * P], xn[:, 4 * k + t, :], ident[:])
                    elif k < 10:
                        b, what = (k - 2) // 4, (k - 2) % 4
                        h = what % 2
                        if what < 2:
                            ins = mm(ps, W[:, OZ + h * P:OZ + (h + 1) * P], hT[:, b, DC - 1:], start=True, stop=True)
                        else:
                            for i in range(DC):
                                o = OTAP + i * DI + h * P
                                ins = mm(ps, W[:, o:o + P], hT[:, b, i:i + L], start=(i == 0), stop=(i == DC - 1))
                    elif k < 12:
                        b = k - 10
                        for h in range(EH):
                            o = OXP + h * NX
                            ins = mm(ps[0:NX], W[:, o:o + NX], xc[:, q, h, b * L:(b + 1) * L],
                                     start=(h == 0), stop=(h == EH - 1))
                    else:
                        b, h = (k - 12) // 2, (k - 12) % 2
                        o = ODT + h * P
                        ins = mm(ps, W[0:RK, o:o + P], dblT[0:RK, b * L:(b + 1) * L], start=True, stop=True)
                    ins.then_inc(hb_full, 1)

                def head_start(v, q):
                    pe.wait_ge(xn_done, v + 1)
                    product(v, q, 0)
                    product(v, q, 1)
                    pe.wait_ge(w_loaded, 16 * v + 16)
                    pe.wait_ge(hb_free, 2 + HEADS * v + 2)
                    product(v, q, 2)
                    product(v, q, 3)

                def head_piece(n, v, q):
                    for k in MAKE_AT.get(n, ()):
                        if k == 10:
                            pe.wait_ge(silu_done, v + 1)
                        if k == 12:
                            pe.wait_ge(hb_free, 2 + HEADS * v + 12)
                        product(v, q, k)

                def project(v, q):
                    pe.wait_ge(yb_ready, v + 1)
                    pe.wait_ge(r_ready, v)
                    for t in range(CT):
                        for h in range(EH):
                            ins = mm(OUT[:, t, :], yb[:, h, t * P:(t + 1) * P],
                                     late[:, q, OOW + h * D:OOW + (h + 1) * D], start=(h == 0), stop=(h == EH - 1))
                    ins.then_inc(out_ready, 1)

                def head0():
                    pe.sem_inc(reduced, RING)
                    pe.wait_ge(zero_pads, 2)
                    head_start(0, 0)
                    for n in range(NST):
                        head_piece(n, 0, 0)

                def body(u, par, tail, head):
                    if head:
                        head_start(u + 1, 1 - par)
                    for n in range(NST):
                        pe.wait_ge(g_made, RING + NST * u + n + 1)
                        if n == 0 and tail:
                            pe.wait_ge(y_read, u)
                        for h in range(EH):
                            for b in range(2):
                                cols = slice(b * L, (b + 1) * L)
                                ins = mm(Y[:, h, cols], ident[:], H[:, n % RING, h, cols],
                                         start=(n == 0), stop=(n == NST - 1))
                        ins.then_inc(reduced, 1)
                        if n == 1 and tail:
                            project(u - 1, 1 - par)
                        if head:
                            head_piece(n, u + 1, 1 - par)

                def tail_last():
                    project(NU - 1, 1)

                units(pe.Fori, head0, body, tail_last)


def build(nc, io, out, phases=3):
    T, D = io["x"].shape
    E, _, F = io["w1"].shape
    CAP = -(-T * 2 * 12 // (E * 10))
    xe_dram = nc.dram_tensor("xe_slots", (E * CAP, D), F32).ap()
    ye_dram = nc.dram_tensor("ye_slots", (E * CAP, D), F32).ap()
    x1_dram = nc.dram_tensor("x1", (T, D), F32).ap()
    r_dram = nc.dram_tensor("r", (3, T, D), F32).ap()
    w = {k: io[k] for k in ("gate_w", "gate_b", "w1", "b1", "w2", "b2")}
    with ExitStack() as ctx:
        def sb(name, shape, dt=F32):
            return ctx.enter_context(nc.sbuf_tensor(name, shape, dt))

        taken = []

        def sem(name):
            taken.append(nc.alloc_semaphore(name))
            return taken[-1]

        def stage_over():
            nc.clear_and_free_semaphores(taken)
            taken.clear()
            nc.all_engine_barrier()

        consts = (sb("ident", [P, P]), sb("ones_b", [P, P], BF16), sb("neg_tri", [P, P], BF16),
                  sb("rev", [P, E]), sb("not_first", [P, E, 8]), sb("neg_half", [P, T // P]),
                  sb("rev_i", [P, E], I32))
        emit_consts(nc, consts, sem)
        if phases == 0:
            emit_moe(nc, 0, T, E, CAP, F, io["x"], None, out, r_dram[0], w, (xe_dram, ye_dram), consts, sem)
            return
        emit_moe(nc, 0, T, E, CAP, F, io["x"], None, x1_dram, r_dram[0], w, (xe_dram, ye_dram), consts, sem)
        stage_over()
        emit_attention(nc, T, D, io, r_dram, consts, sem)
        stage_over()
        emit_moe(nc, 1, T, E, CAP, F, x1_dram, (r_dram[2], io["norm_w"], io["norm_b"]), out, None, w,
                 (xe_dram, ye_dram), consts, sem)


def attention_layout(a, host):
    import numpy as np
    g = {k[len("L0_attn_"):]: v for k, v in a.items() if k.startswith("L0_attn_")}
    NL, E2, D = g["in_proj_w"].shape
    DI = E2 // 2
    EH = DI // P
    NX = g["x_proj_w"].shape[1]
    RK = g["dt_proj_w"].shape[2]

    def halves(m):
        c = m.reshape(NL, DI, -1).shape[2]
        return m.reshape(NL, EH, P, c).transpose(0, 2, 1, 3).reshape(NL, P, EH * c)

    in_T = g["in_proj_w"].transpose(0, 2, 1)
    dt_T = np.zeros((NL, P, DI), np.float32)
    dt_T[:, :RK] = g["dt_proj_w"].transpose(0, 2, 1)
    host["wpack"] = np.concatenate(
        [in_T[:, :, DI:], halves(g["x_proj_w"].transpose(0, 2, 1)), dt_T, g["ln_w"][:, :, None],
         g["ln_b"][:, :, None], halves(g["conv_b"]), halves(g["dt_proj_b"])], axis=2)
    host["late"] = np.concatenate(
        [halves(g["out_proj_w"].transpose(0, 2, 1)), halves(g["A_log"]), halves(g["D_skip"])], axis=2)
    host["in_x"] = in_T[:, :, :DI]
    host["conv_w"] = g["conv_w"].transpose(0, 2, 1)


_PHASES = 3


def kernel(**inputs):
    import numpy as np
    import concourse.bacc as bacc
    from concourse.bass_utils import run_bass_kernel_spmd

    a = {k: np.asarray(v) for k, v in inputs.items()}
    B, S, D = a["L0_attn_x"].shape
    T = B * S
    E, _, F = a["L0_ffn_w1"].shape
    KF = F // P
    host = {
        "x": a["L0_attn_x"].reshape(T, D),
        "gate_w": a["L0_ffn_gate_w"], "gate_b": a["L0_ffn_gate_b"],
        "w1": a["L0_ffn_w1"], "w2": a["L0_ffn_w2"], "b2": a["L0_ffn_b2"],
        "b1": a["L0_ffn_b1"].reshape(E * KF, P).transpose(1, 0),
        "norm_w": a["L0_attn_norm_f_w"], "norm_b": a["L0_attn_norm_f_b"],
    }
    attention_layout(a, host)
    nc = bacc.Bacc("TRN2", target_bir_lowering=False, num_devices=1)
    arrays, io = {}, {}
    for name, v in host.items():
        v = np.ascontiguousarray(v)
        arrays[f"in_{name}"] = v
        io[name] = nc.dram_tensor(f"in_{name}", v.shape, mybir.dt.from_np(v.dtype), kind="ExternalInput").ap()
    out = nc.dram_tensor("out_0", (T, D), F32, kind="ExternalOutput").ap()
    build(nc, io, out, _PHASES)
    res = run_bass_kernel_spmd(nc, [arrays], core_ids=[0])
    return res.results[0]["out_0"].reshape(B, S, D)
```

```python
import concourse.bass as bass
from concourse import mybir
from contextlib import ExitStack

F32 = mybir.dt.float32
BF16 = mybir.dt.bfloat16
I32 = mybir.dt.int32
U32 = mybir.dt.uint32
ALU = mybir.AluOpType
ACT = mybir.ActivationFunctionType
AX_X = mybir.AxisListType.X

P = 128
EPS = 1e-5


def own_wait(eng, spare, s, value):
    eng.wait_ge(s, value)
    eng.sem_inc(spare, 1)


class Chain:

    def __init__(self, eng, sem, base=0):
        self.eng, self.sem, self.base, self.n = eng, sem, base, 0

    def step(self, ins):
        ins.then_inc(self.sem, 1)
        self.n += 1
        return ins

    def wait(self):
        self.eng.wait_ge(self.sem, self.base + self.n)


def emit_consts(nc, consts, named_sem):
    ident, ones_b, neg_tri, rev, not_first, neg_half, rev_i = consts
    made = named_sem("consts_made")
    built = named_sem("consts_built")
    rev_int = named_sem("rev_int")
    with nc.Block() as block:
        @block.gpsimd
        def _(pool):
            ch = Chain(pool, made)
            ch.step(nc.gpsimd.memset(ident[:], 0.0))
            ch.step(nc.gpsimd.memset(neg_tri[:], -1.0))
            ch.step(nc.gpsimd.iota(rev_i[:], pattern=[[-1, rev_i.shape[1]]], base=rev_i.shape[1],
                                   channel_multiplier=0))
            ch.step(nc.gpsimd.memset(ones_b[:], 1.0))
            ch.step(nc.gpsimd.memset(not_first[:], 1.0))
            ch.step(nc.gpsimd.memset(neg_half[:], -0.5))
            ch.wait()
            nc.gpsimd.affine_select(out=ident[:], in_=ident[:], compare_op=ALU.not_equal, fill=1.0, base=0,
                                    pattern=[[-1, P]], channel_multiplier=1).then_inc(built, 1)
            nc.gpsimd.affine_select(out=neg_tri[:], in_=neg_tri[:], compare_op=ALU.is_ge, fill=0.0, base=0,
                                    pattern=[[-1, P]], channel_multiplier=1).then_inc(built, 1)
            nc.gpsimd.memset(not_first[:, :, 0:1], 0.0).then_inc(built, 1)
            nc.gpsimd.tensor_copy(rev[:], rev_i[:]).then_inc(rev_int, 1)
            pool.wait_ge(built, 3)
            pool.wait_ge(rev_int, 1)


def emit_moe(nc, f, T, E, CAP, F, x_src, mix, out_dst, ln_dst, w, scratch, consts, named_sem, packs=None):
    D = P
    NT = T // P
    CT = 8
    NCH = NT // CT
    KF = F // P
    NS = -(-CAP // P)
    LAST = CAP - (NS - 1) * P
    NSLOT = E * CAP
    DW = D + 1
    SKIP = 40000.0
    GT = 8
    NG = NT // GT
    assert SKIP > NSLOT and SKIP > 2 * T and NCH % 2 == 0 and NG % 2 == 0 and E % 2 == 0

    ident, ones_b, neg_tri, rev, not_first, neg_half, _ = consts
    xe_both, y_rows = scratch
    xe_dram = xe_both[f]
    x_v = x_src.rearrange("(c t p) d -> c p t d", p=P, t=CT)

    top = ExitStack()
    with top:
        def sb(name, shape, dt=F32, ctx=top):
            return ctx.enter_context(nc.sbuf_tensor(f"{name}_{f}", shape, dt))

        def sem(name):
            return named_sem(f"{name}_{f}")

        X = sb("X", [P, NT, D])
        gate_wt = sb("gate_wt", [P, NT, 2])
        spare_d = sem("spare_d")
        spare_p = sem("spare_p")
        spare_s = sem("spare_s")

        w1_loaded = [sem("w1_loaded0"), sem("w1_loaded1")]
        w2_loaded = [sem("w2_loaded0"), sem("w2_loaded1")]
        b1_loaded = sem("b1_loaded")
        b2_loaded = sem("b2_loaded")
        w1 = sb("w1", [P, 2, F])
        w2 = sb("w2", [P, 2, KF, D])
        b1 = sb("b1", [P, E * KF])
        b2 = sb("b2", [P, E, D])

        def load_w1(sp, e, par):
            sp.dma_start(w1[:, par, :], w["w1"][e]).then_inc(w1_loaded[par], 16)

        def load_w2(sp, e, par):
            sp.dma_start(w2[:, par], w["w2"][e].rearrange("(k p) d -> p k d", p=P)).then_inc(w2_loaded[par], 16)

        x_loaded = [sem("x_loaded0"), sem("x_loaded1")]
        r_loaded = [sem("r_loaded0"), sem("r_loaded1")]
        x_seen = sem("x_seen")
        r_seen = sem("r_seen")
        x_stats = sem("x_stats")
        r_stats = sem("r_stats")
        mv_done = sem("mv_done")
        rmv_done = sem("rmv_done")
        pool_ln = sem("pool_ln")
        pool_rln = sem("pool_rln")
        zeros_ready = sem("zeros_ready")
        xe_filled = [sem("xe_filled0"), sem("xe_filled1")]
        y_filled = sem("y_filled")
        rows_int = sem("rows_int")
        rows_ready = sem("rows_ready")
        xn_filled = sem("xn_filled")
        nwb_loaded = sem("nwb_loaded")
        rn_ready = sem("rn_ready")
        rn_free = sem("rn_free")
        mixed = sem("mixed")
        xn_ready = sem("xn_ready")
        pt_ready = sem("pt_ready")
        xnT_ready = sem("xnT_ready")
        lg_ready = sem("lg_ready")
        lg_read = sem("lg_read")
        route = sem("route")
        counts_ready = sem("counts_ready")
        pos_ready = sem("pos_ready")
        gap_ready = sem("gap_ready")
        e_ready = sem("e_ready")
        sidx_ready = sem("sidx_ready")
        scattered = [sem("scattered0"), sem("scattered1")]
        gw_loaded = sem("gw_loaded")
        gb_loaded = sem("gb_loaded")
        carry_zero = sem("carry_zero")

        with ExitStack() as c1:
            def sb1(name, shape, dt=F32):
                return sb(name, shape, dt, c1)

            def pb1(name, shape, dt=F32):
                return c1.enter_context(nc.psum_tensor(f"{name}_{f}", shape, dt))

            gate_w = sb1("gate_w", [P, E])
            gate_b = sb1("gate_b", [P, E])
            xg = sb1("xg", [P, 2, CT, D])
            xn = sb1("xn", [P, 2, 2, CT, DW])
            row_i = sb1("row_i", [P, 2, NT], I32)
            row_of = sb1("row_of", [P, 2, NT])
            xnT = sb1("xnT", [P, CT * P])
            L = sb1("L", [P, CT, E])
            L2 = sb1("L2", [P, CT, E])
            eq = sb1("eq", [P, 2, CT, E])
            oh = sb1("oh", [P, 2, CT, E])
            chosen = sb1("chosen", [P, E, CT], BF16)
            counts = sb1("counts", [P, E, CT], BF16)
            carry = sb1("carry", [P, E], BF16)
            top_l = sb1("top_l", [P, 2, CT])
            top_r = sb1("top_r", [P, 2, CT])
            pos = sb1("pos", [P, 2, CT])
            first_slot = sb1("first_slot", [P, 2, CT])
            slot = sb1("slot", [P, 2, CT])
            over = sb1("over", [P, 2, CT])
            keep = sb1("keep", [P, 2, CT])
            gap = sb1("gap", [P, CT])
            egap = sb1("egap", [P, CT])
            den = sb1("den", [P, CT])
            share = sb1("share", [P, 2, CT])
            sidx = sb1("sidx", [P, 2, 2, CT], U32)
            PT = pb1("PT", [P, CT * P])
            LG = pb1("LG", [P, CT, E])
            POS = pb1("POS", [P, E, CT])
            ROUTE_STEPS = 26

            stats = sb1("stats", [P, 2, CT, 6])
            mv = sb1("mv", [P, 2, CT, 2])
            rstd = sb1("rstd", [P, 2, CT])
            nmr = sb1("nmr", [P, 2, CT])
            var_eps = sb1("var_eps", [P, 2, CT])
            neg_mean = sb1("neg_mean", [P, 2, CT])
            if f == 0:
                FQ = max(q for q in range(16, P + 1, 16) if NSLOT % q == 0)
                FR = NSLOT // FQ // 5
                assert FR * 5 * FQ == NSLOT and 2 * T % (8 * P) == 0
                empty = sb1("empty", [FQ, FR, DW])
                zeros = sb1("zeros", [P, 2 * T // (8 * P), D])
                xe_fill = [x.rearrange("(z p r) d -> z p r d", p=FQ, r=FR) for x in xe_both]
                y_fill = y_rows.rearrange("(z p r) d -> z p r d", p=P, z=8)
                fills = ([(xe_fill[0], z, empty, xe_filled[0]) for z in range(5)]
                         + [(y_fill, z, zeros, y_filled) for z in range(8)]
                         + [(xe_fill[1], z, empty, xe_filled[1]) for z in range(5)])
                per = -(-len(fills) // (NCH - 1))
                fill_with = {c: fills[(c - 1) * per:c * per] for c in range(1, NCH)}
            if mix is not None:
                r_src, nw, nb = mix
                r_v = r_src.rearrange("(c t p) d -> c p t d", p=P, t=CT)
                R = sb1("R", [P, NT, D])
                rn = sb1("rn", [P, 2, CT, D])
                nw_b = sb1("nw_b", [P, D])
                nb_b = sb1("nb_b", [P, D])
                r_stat = sb1("r_stat", [P, 2, CT, 6])
                r_mv = sb1("r_mv", [P, 2, CT, 2])
                r_rstd = sb1("r_rstd", [P, 2, CT])
                r_nmr = sb1("r_nmr", [P, 2, CT])

            def steps(fori, step):
                last = NCH // 2 - (1 if mix is None else 2)
                for par in range(2):
                    step(par, 0, par)
                with fori(1, last) as j:
                    for par in range(2):
                        step(2 * j + par, j, par)
                for c in range(2 * last, NCH):
                    step(c, c // 2, c % 2)

            def within(c, ahead):
                return not isinstance(c, int) or c + ahead < NCH

            with nc.Block() as block:
                @block.sync
                def _(sp):
                    for c in range(NCH):
                        j, par = c // 2, c % 2
                        if mix is not None:
                            if c >= 2:
                                sp.wait_ge(r_seen, c - 1)
                            sp.dma_start(R[:, c * CT:(c + 1) * CT, :], r_v[c]).then_inc(r_loaded[par], 16)
                        if c >= 2:
                            sp.wait_ge(x_seen, c - 1)
                        sp.dma_start(X[:, c * CT:(c + 1) * CT, :], x_v[c]).then_inc(x_loaded[par], 16)
                        if c == 0:
                            sp.dma_start(gate_w[:], w["gate_w"]).then_inc(gw_loaded, 16)
                            sp.dma_start(gate_b[:], w["gate_b"].partition_broadcast(P)).then_inc(gb_loaded, 16)
                            if mix is not None:
                                sp.dma_start(nw_b[:], nw.partition_broadcast(P)).then_inc(nwb_loaded, 16)
                                sp.dma_start(nb_b[:], nb.partition_broadcast(P)).then_inc(nwb_loaded, 16)
                        if f == 0 and c > 0:
                            if c == 1:
                                sp.wait_ge(zeros_ready, 3)
                            for dst, z, src, filled in fill_with[c]:
                                sp.dma_start(dst[z], src[:]).then_inc(filled, 16)
                    sp.dma_start(b1[:], w["b1"]).then_inc(b1_loaded, 16)
                    sp.dma_start(b2[:], w["b2"].partition_broadcast(P)).then_inc(b2_loaded, 16)
                    for par in range(2):
                        load_w1(sp, par, par)
                        load_w2(sp, par, par)
                    if f == 0:
                        sp.wait_ge(y_filled, 128)
                        sp.wait_ge(xe_filled[1], 80)

                @block.scalar
                def _(act):
                    def residual_norm(c, par):
                        act.wait_ge(pool_rln, 4 * c + 4)
                        act.wait_ge(rn_free, c + 1)
                        for t in range(CT):
                            k = bass.ds(c * CT + t, 1)
                            ins = nc.scalar.activation(rn[:, par, t, :], R[:, k, :], ACT.Identity,
                                                       bias=r_nmr[:, par, t:t + 1], scale=r_rstd[:, par, t:t + 1])
                        ins.then_inc(rn_ready, 1)

                    def normalise(c, par):
                        act.wait_ge(pool_ln, 4 * c + 4)
                        for t in range(CT):
                            k = bass.ds(c * CT + t, 1)
                            ins = nc.scalar.activation(xg[:, par, t, :], X[:, k, :], ACT.Identity,
                                                       bias=nmr[:, par, t:t + 1], scale=rstd[:, par, t:t + 1])
                        ins.then_inc(xn_ready, 1)

                    def fill_rows(c, j, par):
                        act.wait_ge(xn_ready, c + 1)
                        if not (isinstance(j, int) and j == 0):
                            act.wait_ge(scattered[par], 256 * j)
                        for k in range(2):
                            nc.scalar.copy(xn[:, par, k, :, 0:D], xg[:, par])
                        nc.scalar.copy(xn[:, par, :, :, D], row_of[:, :, bass.ds(c * CT, CT)]
                                       ).then_inc(xn_filled, 1)

                    def step(c, j, par):
                        act.wait_ge(pt_ready, c + 1)
                        act.wait_ge(lg_ready, c + 1)
                        nc.scalar.copy(xnT[:], PT[:]).then_inc(xnT_ready, 1)
                        act.wait_ge(gap_ready, c + 1)
                        nc.scalar.activation(egap[:], gap[:], ACT.Exp).then_inc(e_ready, 1)
                        fill_rows(c, j, par)
                        if within(c, 1):
                            if not (isinstance(c, int) and c == 0):
                                act.wait_ge(xn_filled, c)
                            normalise(c + 1, 1 - par)
                        if mix is not None and within(c, 3):
                            residual_norm(c + 3, 1 - par)

                    act.sem_inc(xnT_ready, 1)
                    act.wait_ge(rows_ready, 1)
                    if mix is not None:
                        act.sem_inc(rn_free, 2)
                        residual_norm(0, 0)
                        residual_norm(1, 1)
                        residual_norm(2, 0)
                    normalise(0, 0)
                    steps(act.Fori, step)

                @block.tensor
                def _(pe):
                    pe.sem_inc(lg_ready, 1)
                    pe.wait_ge(gw_loaded, 16)
                    with pe.Fori(0, NCH // 2) as j:
                        for par in range(2):
                            c = 2 * j + par
                            pe.wait_ge(xn_ready, c + 1)
                            pe.wait_ge(xnT_ready, c + 1)
                            for t in range(CT):
                                ins = nc.tensor.transpose(PT[:, t * P:(t + 1) * P], xg[:, par, t, :], ident[:])
                            ins.then_inc(pt_ready, 1)
                            pe.wait_ge(xnT_ready, c + 2)
                            pe.wait_ge(lg_read, c + 1)
                            for t in range(CT):
                                ins = nc.tensor.matmul(LG[:, t, :], xnT[:, t * P:(t + 1) * P], gate_w[:],
                                                       start=True, stop=True)
                            ins.then_inc(lg_ready, 1)
                            pe.wait_ge(counts_ready, c + 1)
                            flat = "p e t -> p (e t)"
                            nc.tensor.matmul(POS[:].rearrange(flat), ones_b[:], counts[:].rearrange(flat),
                                             start=True, stop=False)
                            nc.tensor.matmul(POS[:], ones_b[:],
                                             carry[:].unsqueeze(2).to_broadcast([P, E, CT]),
                                             start=False, stop=False)
                            nc.tensor.matmul(POS[:].rearrange(flat), neg_tri[:], chosen[:].rearrange(flat),
                                             start=False, stop=True).then_inc(pos_ready, 1)

                @block.vector
                def _(dve):
                    v = nc.vector
                    ch0 = Chain(dve, carry_zero)
                    ch0.step(v.memset(carry[:], 0.0))
                    ch0.wait()
                    dve.sem_inc(lg_read, 1)
                    dve.wait_ge(gb_loaded, 16)
                    bce = [P, CT, E]

                    def per_token(a):
                        return a.unsqueeze(2).to_broadcast(bce)

                    rev_b = rev[:].unsqueeze(1).to_broadcast(bce)

                    def statistics(src, st, dst, st_done, done, used, c, j, par):
                        if not (isinstance(j, int) and j == 0):
                            own_wait(dve, spare_d, used, 4 * c - 4)
                        for t in range(CT):
                            ins = nc.vector.bn_stats(st[:, par, t, :], src[:, bass.ds(c * CT + t, 1), :])
                        ins.then_inc(st_done, 1)
                        own_wait(dve, spare_d, st_done, c + 1)
                        for t in range(CT):
                            ins = nc.vector.bn_aggr(dst[:, par, t, :], st[:, par, t, :])
                        ins.then_inc(done, 1)

                    def residual_part(c, j, par):
                        own_wait(dve, spare_d, r_loaded[par], 16 * j + 16)
                        statistics(R, r_stat, r_mv, r_stats, rmv_done, pool_rln, c, j, par)
                        dve.sem_inc(r_seen, 1)

                    def mix_and_statistics(c, j, par):
                        own_wait(dve, spare_d, x_loaded[par], 16 * j + 16)
                        if mix is not None:
                            dve.wait_ge(rn_ready, c + 1)
                            ch = Chain(dve, mixed, 3 * c)
                            rp = rn[:, par]
                            ch.step(nc.vector.tensor_tensor(
                                rp, rp, nw_b[:].unsqueeze(1).to_broadcast([P, CT, D]), ALU.mult))
                            ch.wait()
                            ch.step(nc.vector.tensor_tensor(
                                rp, rp, nb_b[:].unsqueeze(1).to_broadcast([P, CT, D]), ALU.add))
                            ch.wait()
                            xc = X[:, bass.ds(c * CT, CT), :]
                            ch.step(nc.vector.tensor_tensor(xc, xc, rp, ALU.add))
                            ch.wait()
                            dve.sem_inc(rn_free, 1)
                        statistics(X, stats, mv, x_stats, mv_done, pool_ln, c, j, par)
                        dve.sem_inc(x_seen, 1)

                    def step(c, j, par):
                        if mix is not None and within(c, 3):
                            residual_part(c + 3, j + 1 + par, 1 - par)
                        if within(c, 2):
                            mix_and_statistics(c + 2, j + 1, par)
                        ch = Chain(dve, route, ROUTE_STEPS * c)
                        dve.wait_ge(lg_ready, c + 2)
                        ch.step(v.tensor_tensor(L[:], LG[:], gate_b[:].unsqueeze(1).to_broadcast(bce), ALU.add))
                        ch.wait()
                        dve.sem_inc(lg_read, 1)
                        for k, src in ((0, L), (1, L2)):
                            ch.step(v.tensor_reduce(top_l[:, k, :], src[:], AX_X, ALU.max))
                            ch.wait()
                            ch.step(v.tensor_tensor(eq[:, k], src[:], per_token(top_l[:, k, :]), ALU.is_equal))
                            ch.wait()
                            ch.step(v.tensor_tensor(eq[:, k], eq[:, k], rev_b, ALU.mult))
                            ch.wait()
                            ch.step(v.tensor_reduce(top_r[:, k, :], eq[:, k], AX_X, ALU.max))
                            ch.wait()
                            ch.step(v.tensor_tensor(oh[:, k], rev_b, per_token(top_r[:, k, :]), ALU.is_equal))
                            ch.wait()
                            if k == 0:
                                ch.step(v.scalar_tensor_tensor(L2[:], oh[:, 0], -3e38, L[:],
                                                               ALU.mult, ALU.add))
                                ch.wait()
                        ch.step(v.tensor_tensor(chosen[:].rearrange("p e t -> p t e"), oh[:, 0], oh[:, 1],
                                                ALU.add))
                        ch.step(v.tensor_tensor(gap[:], top_l[:, 1, :], top_l[:, 0, :], ALU.subtract))
                        ch.wait()
                        dve.sem_inc(gap_ready, 1)
                        v.tensor_tensor_scan(counts[:].rearrange("p e t -> p (e t)"),
                                             not_first[:].rearrange("p e t -> p (e t)"),
                                             chosen[:].rearrange("p e t -> p (e t)"), 0.0,
                                             ALU.mult, ALU.add).then_inc(counts_ready, 1)
                        ch.step(v.tensor_scalar(first_slot[:], top_r[:], float(-CAP), float(E * CAP),
                                                ALU.mult, ALU.add))
                        dve.wait_ge(e_ready, c + 1)
                        ch.step(v.tensor_scalar(den[:], egap[:], 1.0, None, ALU.add))
                        ch.wait()
                        ch.step(v.reciprocal(share[:, 0, :], den[:]))
                        ch.wait()
                        ch.step(v.tensor_tensor(share[:, 1, :], share[:, 0, :], egap[:], ALU.mult))
                        dve.wait_ge(pos_ready, c + 1)
                        ch.step(v.tensor_tensor(eq[:, 0], oh[:, 0], POS[:].rearrange("p e t -> p t e"),
                                                ALU.mult))
                        ch.step(v.tensor_tensor(eq[:, 1], oh[:, 1], POS[:].rearrange("p e t -> p t e"),
                                                ALU.mult))
                        ch.step(v.tensor_tensor(carry[:], carry[:], counts[:, :, CT - 1], ALU.add))
                        ch.wait()
                        ch.step(v.tensor_reduce(pos[:], eq[:], AX_X, ALU.add))
                        ch.wait()
                        ch.step(v.tensor_tensor(slot[:], first_slot[:], pos[:], ALU.add))
                        ch.step(v.tensor_scalar(over[:], pos[:], float(CAP), None, ALU.is_ge))
                        ch.step(v.tensor_scalar(keep[:], pos[:], float(CAP), 0.5, ALU.is_lt, ALU.mult))
                        ch.wait()
                        if not (isinstance(j, int) and j == 0):
                            dve.wait_ge(scattered[par], 256 * j)
                        v.scalar_tensor_tensor(sidx[:, par], over[:], SKIP, slot[:],
                                               ALU.mult, ALU.add).then_inc(sidx_ready, 1)
                        tiles = bass.ds(c * CT, CT)
                        ch.step(v.tensor_tensor(gate_wt[:, tiles, :].rearrange("p t k -> p k t"),
                                                share[:], keep[:], ALU.mult))
                        assert ch.n == ROUTE_STEPS, ch.n
                        ch.wait()

                    if mix is not None:
                        dve.wait_ge(nwb_loaded, 32)
                        residual_part(0, 0, 0)
                        residual_part(1, 0, 1)
                    mix_and_statistics(0, 0, 0)
                    if mix is not None:
                        residual_part(2, 1, 0)
                    mix_and_statistics(1, 0, 1)
                    steps(dve.Fori, step)

                @block.gpsimd
                def _(pool):
                    def norm_scalars(stat, rs, nr, done, used, made, c, j, par):
                        own_wait(pool, spare_p, done, c + 1)
                        if not (isinstance(j, int) and j == 0):
                            own_wait(pool, spare_p, used, c - 1)
                        ve, nm = var_eps[:, par], neg_mean[:, par]
                        ch = Chain(pool, made, 4 * c)
                        ch.step(nc.gpsimd.tensor_scalar(ve, stat[:, par, :, 1], EPS, None, ALU.add))
                        ch.step(nc.gpsimd.tensor_scalar(nm, stat[:, par, :, 0], -1.0, None, ALU.mult))
                        ch.wait()
                        ch.step(nc.gpsimd.tensor_tensor(rs[:, par], ve, neg_half[:, 0:CT], ALU.pow))
                        ch.wait()
                        ch.step(nc.gpsimd.tensor_tensor(nr[:, par], nm, rs[:, par], ALU.mult))
                        ch.wait()

                    def residual_scalars(c, j, par):
                        norm_scalars(r_mv, r_rstd, r_nmr, rmv_done, rn_ready, pool_rln, c, j, par)

                    def token_scalars(c, j, par):
                        norm_scalars(mv, rstd, nmr, mv_done, xn_ready, pool_ln, c, j, par)

                    def step(c, j, par):
                        if mix is not None and within(c, 3):
                            residual_scalars(c + 3, j + 1 + par, 1 - par)
                        if within(c, 2):
                            token_scalars(c + 2, j + 1, par)
                        if f == 0 and isinstance(c, int) and c == 0:
                            pool.wait_ge(xe_filled[0], 80)
                        own_wait(pool, spare_p, xn_filled, c + 1)
                        own_wait(pool, spare_p, sidx_ready, c + 1)
                        for t in range(CT):
                            for k in range(2):
                                nc.gpsimd.indirect_dma_start(
                                    out=xe_dram, in_=xn[:, par, k, t, :], in_offset=None,
                                    out_offset=bass.IndirectOffsetOnAxis(ap=sidx[:, par, k, t:t + 1], axis=0),
                                    bounds_check=NSLOT - 1, oob_is_err=False).then_inc(scattered[par], 16)

                    if f == 0:
                        nc.gpsimd.memset(empty[:, :, 0:D], 0.0).then_inc(zeros_ready, 1)
                        nc.gpsimd.memset(empty[:, :, D:DW], SKIP).then_inc(zeros_ready, 1)
                        nc.gpsimd.memset(zeros[:], 0.0).then_inc(zeros_ready, 1)
                    nc.gpsimd.iota(row_i[:], pattern=[[T, 2], [P, NT]], base=0,
                                   channel_multiplier=1).then_inc(rows_int, 1)
                    pool.wait_ge(rows_int, 1)
                    nc.gpsimd.tensor_copy(row_of[:], row_i[:]).then_inc(rows_ready, 1)
                    if mix is not None:
                        residual_scalars(0, 0, 0)
                        residual_scalars(1, 0, 1)
                    token_scalars(0, 0, 0)
                    if mix is not None:
                        residual_scalars(2, 1, 0)
                    token_scalars(1, 0, 1)
                    steps(pool.Fori, step)
                    for par in range(2):
                        pool.wait_ge(scattered[par], 256 * (NCH // 2))

        xe_loaded = [sem("xe_loaded0"), sem("xe_loaded1")]
        xt_ready = sem("xt_ready")
        xt_copied = sem("xt_copied")
        h_ready = sem("h_ready")
        g_ready = sem("g_ready")
        y_ready = sem("y_ready")
        y_copied = sem("y_copied")
        rows_out_ready = sem("rows_out_ready")
        y_scattered = [sem("y_scattered0"), sem("y_scattered1")]

        with ExitStack() as c2:
            def sb2(name, shape, dt=F32):
                return sb(name, shape, dt, c2)

            def pb2(name, shape, dt=F32):
                return c2.enter_context(nc.psum_tensor(f"{name}_{f}", shape, dt))

            xe = sb2("xe", [P, 2, NS, DW])
            rows_out = sb2("rows_out", [P, 2, NS], U32)
            xeT = sb2("xeT", [P, 2, NS * P])
            hT = sb2("hT", [P, 2, KF, CAP])
            ye = sb2("ye", [P, 2, NS, D])
            XT = pb2("XT", [P, 1024])
            H = pb2("H", [P, 2, 1024])
            Y = pb2("Y", [P, 1024])
            early = None if packs is None else PackWork(nc, packs, ident, sb2, sem)
            SLOTS = [(s * P, P if s < NS - 1 else LAST) for s in range(NS)]
            FULL = (NS - 1) * P

            def experts(fori, step):
                for par in range(2):
                    step(par, 0, par)
                with fori(1, E // 2 - 1) as j:
                    for par in range(2):
                        step(2 * j + par, j, par)
                for par in range(2):
                    step(E - 2 + par, E // 2 - 1, par)

            def within(e, ahead):
                return not isinstance(e, int) or e + ahead < E

            with nc.Block() as block:
                @block.sync
                def _(sp):
                    def load_xe(e, par):
                        rows = xe_dram[bass.ds(e * CAP, CAP), :]
                        sp.dma_start(xe[:, par, 0:NS - 1, :],
                                     rows[0:FULL, :].rearrange("(s p) d -> p s d", p=P)
                                     ).then_inc(xe_loaded[par], 16)
                        sp.dma_start(xe[0:LAST, par, NS - 1, :], rows[FULL:CAP, :]
                                     ).then_inc(xe_loaded[par], 16)

                    def step(e, j, par):
                        if within(e, 2):
                            own_wait(sp, spare_s, rows_out_ready, e + 1)
                            load_xe(e + 2, par)
                            own_wait(sp, spare_s, h_ready, KF * e + KF)
                            load_w1(sp, e + 2, par)
                            own_wait(sp, spare_s, y_ready, e + 1)
                            load_w2(sp, e + 2, par)

                    load_xe(0, 0)
                    load_xe(1, 1)
                    if early is not None:
                        early.load(sp)
                    experts(sp.Fori, step)
                    if early is not None:
                        early.store(sp)

                @block.tensor
                def _(pe):
                    def transposes(e, j, par):
                        pe.wait_ge(xe_loaded[par], 32 * j + 32)
                        pe.wait_ge(xt_copied, e + 1)
                        for s, (at, n) in enumerate(SLOTS):
                            ins = nc.tensor.transpose(XT[:, at:at + n], xe[0:n, par, s, 0:D], ident[0:n, 0:n])
                        ins.then_inc(xt_ready, 1)

                    def step(e, j, par):
                        pe.wait_ge(xt_copied, e + 2)
                        pe.wait_ge(w1_loaded[par], 16 * j + 16)
                        for k in range(KF):
                            pe.wait_ge(g_ready, KF * e + k + 1)
                            for a, b in ((0, 512), (512, CAP)):
                                ins = nc.tensor.matmul(H[:, k % 2, a:b], w1[:, par, k * P:(k + 1) * P],
                                                       xeT[:, par, a:b], start=True, stop=True)
                            ins.then_inc(h_ready, 1)
                        if within(e, 1):
                            transposes(e + 1, j + par, 1 - par)
                        pe.wait_ge(g_ready, 2 + KF * e + KF)
                        pe.wait_ge(w2_loaded[par], 16 * j + 16)
                        pe.wait_ge(y_copied, e + 1)
                        for s, (at, n) in enumerate(SLOTS):
                            for k in range(KF):
                                ins = nc.tensor.matmul(Y[0:n, s * D:(s + 1) * D], hT[:, par, k, at:at + n],
                                                       w2[:, par, k, :], start=(k == 0), stop=(k == KF - 1))
                        ins.then_inc(y_ready, 1)

                    transposes(0, 0, 0)
                    experts(pe.Fori, step)

                @block.scalar
                def _(act):
                    def step(e, j, par):
                        if not (isinstance(j, int) and j == 0):
                            act.wait_ge(y_ready, e - 1)
                        for k in range(KF):
                            act.wait_ge(h_ready, KF * e + k + 1)
                            nc.scalar.activation(hT[:, par, k, :], H[:, k % 2, 0:CAP], ACT.Gelu,
                                                 bias=b1[:, bass.ds(e * KF + k, 1)]).then_inc(g_ready, 1)

                    act.sem_inc(g_ready, 2)
                    if early is not None:
                        early.exponentiate(act)
                    act.wait_ge(b1_loaded, 16)
                    experts(act.Fori, step)

                @block.vector
                def _(dve):
                    def copy_tokens(e, j, par):
                        dve.wait_ge(xt_ready, e + 1)
                        if not (isinstance(j, int) and j == 0):
                            dve.wait_ge(h_ready, KF * e - KF)
                        nc.vector.tensor_copy(xeT[:, par, 0:CAP], XT[:, 0:CAP]).then_inc(xt_copied, 1)
                        if not (isinstance(j, int) and j == 0):
                            dve.wait_ge(y_scattered[par], 16 * NS * j)
                        nc.vector.tensor_copy(rows_out[:, par, 0:NS - 1], xe[:, par, 0:NS - 1, D])
                        nc.vector.tensor_copy(rows_out[0:LAST, par, NS - 1:NS], xe[0:LAST, par, NS - 1:NS, D]
                                              ).then_inc(rows_out_ready, 1)

                    def step(e, j, par):
                        if within(e, 1):
                            copy_tokens(e + 1, j + par, 1 - par)
                        dve.wait_ge(y_ready, e + 1)
                        bias = b2[:, bass.ds(e, 1), :]
                        nc.vector.tensor_tensor(
                            ye[:, par, 0:NS - 1, :], Y[:, 0:FULL].rearrange("p (s d) -> p s d", d=D),
                            bias.to_broadcast([P, NS - 1, D]), ALU.add)
                        nc.vector.tensor_tensor(
                            ye[0:LAST, par, NS - 1:NS, :],
                            Y[0:LAST, FULL:FULL + D].rearrange("p (s d) -> p s d", d=D),
                            bias[0:LAST], ALU.add).then_inc(y_copied, 1)

                    dve.sem_inc(xt_copied, 1)
                    dve.sem_inc(y_copied, 1)
                    dve.wait_ge(b2_loaded, 16)
                    copy_tokens(0, 0, 0)
                    if early is not None:
                        early.fold(dve)
                    experts(dve.Fori, step)

                @block.gpsimd
                def _(pool):
                    def step(e, j, par):
                        own_wait(pool, spare_p, rows_out_ready, e + 1)
                        own_wait(pool, spare_p, y_copied, e + 2)
                        for s, (at, n) in enumerate(SLOTS):
                            nc.gpsimd.indirect_dma_start(
                                out=y_rows, in_=ye[0:n, par, s, :], in_offset=None,
                                out_offset=bass.IndirectOffsetOnAxis(ap=rows_out[0:n, par, s:s + 1], axis=0),
                                bounds_check=2 * T - 1, oob_is_err=False).then_inc(y_scattered[par], 16)

                    experts(pool.Fori, step)
                    for par in range(2):
                        pool.wait_ge(y_scattered[par], 16 * NS * (E // 2))

        y_loaded = [sem("y_loaded0"), sem("y_loaded1")]
        summed = sem("summed")
        out_stored = [sem("out_stored0"), sem("out_stored1")]
        group_stats = sem("group_stats")
        group_mv = sem("group_mv")
        group_scalars = sem("group_scalars")
        ln_ready = sem("ln_ready")
        ln_stored = [sem("ln_stored0"), sem("ln_stored1")]

        with ExitStack() as c3:
            def sb3(name, shape, dt=F32):
                return sb(name, shape, dt, c3)

            yk = sb3("yk", [P, 2, 2, GT, D])
            xo = sb3("xo", [P, 2, GT, D])
            gstat = sb3("gstat", [P, 2, GT, 6])
            gmv = sb3("gmv", [P, 2, GT, 2])
            gve = sb3("gve", [P, 2, GT])
            gnm = sb3("gnm", [P, 2, GT])
            grstd = sb3("grstd", [P, 2, GT])
            gnmr = sb3("gnmr", [P, 2, GT])
            xln = sb3("xln", [P, 2, GT, D])
            y_v = y_rows.rearrange("(k g t p) d -> g k p t d", k=2, p=P, t=GT)
            out_v = out_dst.rearrange("(g t p) d -> g p t d", p=P, t=GT)
            ln_v = None if ln_dst is None else ln_dst.rearrange("(g t p) d -> g p t d", p=P, t=GT)

            with nc.Block() as block:
                @block.sync
                def _(sp):
                    for par in range(2):
                        sp.sem_inc(out_stored[par], 16)
                    for g in range(NG):
                        if g >= 2:
                            sp.wait_ge(summed, 2 * g - 2)
                            sp.dma_start(out_v[g - 2], xo[:, g % 2]).then_inc(out_stored[g % 2], 16)
                        for k in range(2):
                            sp.dma_start(yk[:, g % 2, k], y_v[g, k]).then_inc(y_loaded[g % 2], 16)
                    for g in (NG - 2, NG - 1):
                        sp.wait_ge(summed, 2 * g + 2)
                        sp.dma_start(out_v[g], xo[:, g % 2]).then_inc(out_stored[g % 2], 16)
                    for par in range(2):
                        sp.wait_ge(out_stored[par], 16 * (NG // 2) + 16)

                @block.vector
                def _(dve):
                    with dve.Fori(0, NG // 2) as j:
                        for par in range(2):
                            g = 2 * j + par
                            dve.wait_ge(y_loaded[par], 32 * j + 32)
                            dve.wait_ge(out_stored[par], 16 * j + 16)
                            if ln_dst is not None:
                                dve.wait_ge(ln_ready, g + 1)
                            ch = Chain(dve, summed, 2 * g)
                            for k in range(2):
                                for t in range(GT):
                                    tile = bass.ds(g * GT + t, 1)
                                    src = X[:, tile, :] if k == 0 else xo[:, par, t:t + 1, :]
                                    ins = nc.vector.scalar_tensor_tensor(
                                        xo[:, par, t:t + 1, :], yk[:, par, k, t:t + 1, :],
                                        gate_wt[:, tile, k], src, ALU.mult, ALU.add)
                                ch.step(ins)
                                ch.wait()
                            if ln_dst is not None:
                                dve.wait_ge(group_scalars, 4 * g + 4)
                                for t in range(GT):
                                    ins = nc.vector.bn_stats(gstat[:, par, t, :], xo[:, par, t, :])
                                ins.then_inc(group_stats, 1)
                                own_wait(dve, spare_d, group_stats, g + 1)
                                for t in range(GT):
                                    ins = nc.vector.bn_aggr(gmv[:, par, t, :], gstat[:, par, t, :])
                                ins.then_inc(group_mv, 1)

                if ln_dst is not None:
                    @block.gpsimd
                    def _(pool):
                        pool.sem_inc(group_scalars, 8)
                        with pool.Fori(0, NG // 2) as j:
                            for par in range(2):
                                g = 2 * j + par
                                own_wait(pool, spare_p, group_mv, g + 1)
                                own_wait(pool, spare_p, ln_ready, g + 1)
                                ch = Chain(pool, group_scalars, 8 + 4 * g)
                                ch.step(nc.gpsimd.tensor_scalar(gve[:, par], gmv[:, par, :, 1], EPS, None, ALU.add))
                                ch.step(nc.gpsimd.tensor_scalar(gnm[:, par], gmv[:, par, :, 0], -1.0, None,
                                                                ALU.mult))
                                ch.wait()
                                ch.step(nc.gpsimd.tensor_tensor(grstd[:, par], gve[:, par], neg_half[:, 0:GT],
                                                                ALU.pow))
                                ch.wait()
                                ch.step(nc.gpsimd.tensor_tensor(gnmr[:, par], gnm[:, par], grstd[:, par],
                                                                ALU.mult))
                                ch.wait()

                    @block.scalar
                    def _(act):
                        act.sem_inc(ln_ready, 2)
                        for par in range(2):
                            act.sem_inc(ln_stored[par], 16)
                        with act.Fori(0, NG // 2) as j:
                            for par in range(2):
                                g = 2 * j + par
                                act.wait_ge(group_scalars, 8 + 4 * g + 4)
                                act.wait_ge(ln_stored[par], 16 * j + 16)
                                for t in range(GT):
                                    ins = nc.scalar.activation(xln[:, par, t, :], xo[:, par, t, :], ACT.Identity,
                                                               bias=gnmr[:, par, t:t + 1],
                                                               scale=grstd[:, par, t:t + 1])
                                ins.then_inc(ln_ready, 1)
                                act.wait_ge(ln_ready, 2 + g + 1)
                                act.dma_start(ln_v[g], xln[:, par]).then_inc(ln_stored[par], 16)
                        for par in range(2):
                            act.wait_ge(ln_stored[par], 16 * (NG // 2) + 16)


class Packs:

    def __init__(self, nc, D, io):
        self.io = io
        self.NL = io["wpack"].shape[0]
        self.EH = 2
        self.DI = self.EH * P
        self.DC = 4
        self.NST = 16
        self.RK = D // 16
        self.NX = self.RK + 2 * self.NST
        self.OZ = 0
        self.OTAP = self.OZ + self.DI
        self.OXP = self.OTAP + self.DC * self.DI
        self.ODT = self.OXP + self.EH * self.NX
        self.OLW = self.ODT + self.DI
        self.OLB = self.OLW + 1
        self.OCB = self.OLB + 1
        self.ODB = self.OCB + self.EH
        self.NW = self.ODB + self.EH
        self.OOW = 0
        self.OA = self.OOW + self.EH * D
        self.OD = self.OA + self.EH * self.NST
        self.ODG = self.OD + self.EH
        self.NLATE = self.ODG + self.EH * P
        self.heads = nc.dram_tensor("head_pack", (self.NL, P, self.NW), F32).ap()
        self.late = nc.dram_tensor("late_pack", (self.NL, P, self.NLATE), F32).ap()


class PackWork:

    def __init__(self, nc, packs, ident, sb, sem):
        p = self.p = packs
        self.nc, self.ident = nc, ident
        self.raw_loaded = sem("raw_loaded")
        self.a_exp = sem("a_exp")
        self.folded = sem("folded")
        self.pack_stored = sem("pack_stored")
        self.pk = sb("pk", [P, p.NL, p.NW])
        self.lt = sb("lt", [P, p.NL, p.NLATE])
        self.in_x = sb("in_x", [P, p.NL, p.DI])
        self.taps = sb("taps", [P, p.NL, p.DC, p.DI])

    def load(self, sp):
        p, io = self.p, self.p.io
        for l in range(p.NL):
            for dst, src in ((self.pk[:, l, p.OZ:p.OTAP], io["wpack"][l, :, 0:p.DI]),
                             (self.pk[:, l, p.OXP:p.NW], io["wpack"][l, :, p.DI:]),
                             (self.lt[:, l, 0:p.ODG], io["late"][l]),
                             (self.in_x[:, l, :], io["in_x"][l]),
                             (self.taps[:, l], io["conv_w"][l].partition_broadcast(P))):
                sp.dma_start(dst, src).then_inc(self.raw_loaded, 16)

    def exponentiate(self, act):
        p = self.p
        act.wait_ge(self.raw_loaded, 80 * p.NL)
        a = self.lt[:, :, p.OA:p.OD]
        self.nc.scalar.activation(a, a, ACT.Exp).then_inc(self.a_exp, 1)

    def fold(self, dve):
        p, v = self.p, self.nc.vector
        dve.wait_ge(self.raw_loaded, 80 * p.NL)
        for l in range(p.NL):
            v.tensor_tensor(
                self.pk[:, l, p.OTAP:p.OXP].rearrange("p (k e) -> p k e", k=p.DC), self.taps[:, l],
                self.in_x[:, l, :].unsqueeze(1).to_broadcast([P, p.DC, p.DI]), ALU.mult)
            v.tensor_tensor(
                self.lt[:, l, p.ODG:p.NLATE].rearrange("p (h c) -> p h c", h=p.EH),
                self.lt[:, l, p.OD:p.ODG].unsqueeze(2).to_broadcast([P, p.EH, P]),
                self.ident[:].unsqueeze(1).to_broadcast([P, p.EH, P]), ALU.mult).then_inc(self.folded, 1)
        dve.wait_ge(self.a_exp, 1)
        for l in range(p.NL):
            a = self.lt[:, l, p.OA:p.OD]
            v.tensor_scalar(a, a, -1.0, None, ALU.mult).then_inc(self.folded, 1)

    def store(self, sp):
        p = self.p
        sp.wait_ge(self.folded, 2 * p.NL)
        for l in range(p.NL):
            sp.dma_start(p.heads[l], self.pk[:, l, :]).then_inc(self.pack_stored, 16)
            sp.dma_start(p.late[l], self.lt[:, l, :]).then_inc(self.pack_stored, 16)
        sp.wait_ge(self.pack_stored, 32 * p.NL)


def emit_attention(nc, T, L, D, packs, r_dram, consts, named_sem):
    ident, neg_half = consts[0], consts[5]
    NL, EH, DI, DC, NST, RK, NX = packs.NL, packs.EH, packs.DI, packs.DC, packs.NST, packs.RK, packs.NX
    OZ, OTAP, OXP, ODT, OLW, OLB, OCB, ODB = (packs.OZ, packs.OTAP, packs.OXP, packs.ODT, packs.OLW, packs.OLB,
                                              packs.OCB, packs.ODB)
    OOW, OA, ODG = packs.OOW, packs.OA, packs.ODG
    pack_dram, late_dram = packs.heads, packs.late
    U = 2 * L
    CT = U // P
    NPAIR = T // U
    NU = NL * NPAIR
    RING = 4
    HEADS = 16
    ON_POOL = (0, 2, 3, 5, 7, 8, 10, 12, 13, 14)
    ON_DVE = tuple(n for n in range(NST) if n not in ON_POOL)
    MAKE_AT = {0: (2, 3), 1: (4,), 2: (5, 6), 3: (7, 8), 4: (9,), 8: (10, 11), 9: (12, 13, 14, 15)}
    PROJECT_AT, ADD_AT = 5, 9
    EVICT_AT = {2: (0, 1), 4: (2, 3), 5: (4,), 6: (5, 6), 7: (7, 8), 8: (9,), 11: (10, 11),
                12: (12, 13), 13: (14, 15)}
    bc_dram = nc.dram_tensor("bc_rows", (2, 2 * NST, U), F32).ap()

    top = ExitStack()
    with top:
        def sb(name, shape, dt=F32, ctx=top):
            return ctx.enter_context(nc.sbuf_tensor(name, shape, dt))

        def sem(name):
            return named_sem(name)

        W = sb("W", [P, packs.NW])
        late = sb("late", [P, 2, packs.NLATE])
        r_head = sb("r_head", [P, CT, D])
        r_tail = sb("r_tail", [P, CT, D])
        hstat = sb("hstat", [P, CT, 6])
        hmv = sb("hmv", [P, CT, 2])
        h_ve = sb("h_ve", [P, CT])
        h_nm = sb("h_nm", [P, CT])
        h_rstd = sb("h_rstd", [P, CT])
        h_nmr = sb("h_nmr", [P, CT])
        xn = sb("xn_a", [P, CT, D])
        hT = sb("hT_a", [P, 2, DC - 1 + L])
        xc = sb("xc", [P, 2, EH, U])
        zs = sb("zs", [P, 2, EH, U])
        dt = sb("dt", [P, 2, EH, U])
        dtx = sb("dtx", [P, 2, EH, U])
        dblT = sb("dblT", [NX, U])
        yb = sb("yb", [P, EH, U])
        ln_u = sb("ln_u", [P, EH, U])
        dA = sb("dA", [P, 2, EH, 2, L])
        H = sb("Hst", [P, RING, EH, U])
        Bb = sb("Bb", [P, RING, U])
        Cb = sb("Cb", [P, RING, U])
        Y = top.enter_context(nc.psum_tensor("Y_a", [P, EH, U], F32))
        HB = top.enter_context(nc.psum_tensor("HB_a", [P, 2, 512], F32))
        DBX = top.enter_context(nc.psum_tensor("DBX", [P, U], F32))

        w_loaded = sem("w_loaded")
        late_loaded = sem("late_loaded")
        rh_loaded = sem("rh_loaded")
        rt_loaded = sem("rt_loaded")
        r_stored = sem("r_stored")
        B_loaded = [sem(f"B_loaded{i}") for i in range(RING)]
        C_loaded = [sem(f"C_loaded{i}") for i in range(RING)]
        bc_stored = sem("bc_stored")
        hst_done = sem("hst_done")
        hmv_ready = sem("hmv_ready")
        hscal = sem("hscal")
        xn_done = sem("xn_done")
        hb_full = sem("hb_full")
        hb_free = sem("hb_free")
        silu_done = sem("silu_done")
        exp_done = sem("exp_done")
        ln_done = sem("ln_done")
        one_u = sem("one_u")
        ln_exact = sem("ln_exact")
        lost_ready = sem("lost_ready")
        dt_half = sem("dt_half")
        dt_ready = sem("dt_ready")
        dtx_ready = sem("dtx_ready")
        dA_ready = sem("dA_ready")
        dbu = sem("dbu")
        scanned = sem("scanned")
        g_pool = sem("g_pool")
        g_dve = sem("g_dve")
        reduced = sem("reduced")
        yb_ready = sem("yb_ready")
        out_ready = sem("out_ready")
        r_ready = sem("r_ready")
        zero_pads = sem("zero_pads")
        spare_d = sem("spare_d")
        spare_p = sem("spare_p")
        spare_s = sem("spare_s")

        r_units = r_dram.rearrange("l (u t p) d -> (l u) p t d", p=P, t=CT)

        def h_times_c(u, n):
            sem_, mine = (g_pool, ON_POOL) if n % NST in ON_POOL else (g_dve, ON_DVE)
            return sem_, len(mine) * (u + (1 if n >= 0 else 0)) + mine.index(n % NST) + 1

        def more(u):
            return not isinstance(u, int) or u + 2 < NU

        def units(fori, head0, body, tail_last):
            head0()
            body(0, 0, False, True)
            body(1, 1, True, True)
            with fori(1, NU // 2 - 1) as j:
                for par in range(2):
                    body(2 * j + par, par, True, True)
            body(NU - 2, 0, True, True)
            body(NU - 1, 1, True, False)
            tail_last()

        with nc.Block() as block:
            @block.sync
            def _(sp):
                def load_weights(v):
                    sp.wait_ge(hb_free, HEADS * v + 2)
                    sp.dma_start(W[:], pack_dram[v // NPAIR]).then_inc(w_loaded, 16)

                def load_late(v, q):
                    sp.dma_start(late[:, q, :], late_dram[v // NPAIR]).then_inc(late_loaded, 16)

                def load_head_residual(v):
                    own_wait(sp, spare_s, xn_done, v)
                    own_wait(sp, spare_s, r_stored, 16 * v + 16)
                    sp.dma_start(r_head[:], r_units[v]).then_inc(rh_loaded, 16)

                def store_residual(v):
                    own_wait(sp, spare_s, r_ready, 2 * v + 2)
                    sp.dma_start(r_units[v + NPAIR], r_tail[:]).then_inc(r_stored, 16)

                def head0():
                    sp.sem_inc(r_stored, 16 * NPAIR)
                    load_weights(0)
                    load_late(0, 0)
                    load_head_residual(0)
                    load_head_residual(1)
                    load_weights(1)

                def body(u, par, tail, head):
                    own_wait(sp, spare_s, bc_stored, 16 * u + 16)
                    for n in range(NST):
                        s = n % RING
                        sp.wait_ge(dbu, EH * (NST * u + n + 1))
                        sp.dma_start(Bb[:, s, :], bc_dram[par, n].partition_broadcast(P)).then_inc(B_loaded[s], 16)
                        sp.wait_ge(*h_times_c(u, n - RING))
                        sp.dma_start(Cb[:, s, :], bc_dram[par, NST + n].partition_broadcast(P)
                                     ).then_inc(C_loaded[s], 16)
                        if n == 4 and more(u):
                            load_head_residual(u + 2)
                        if n == 14 and head:
                            if tail:
                                own_wait(sp, spare_s, out_ready, 2 * u)
                            load_late(u + 1, 1 - par)
                        if n == 15:
                            if tail:
                                store_residual(u - 1)
                            own_wait(sp, spare_s, r_stored, 16 * NPAIR + 16 * u)
                            sp.dma_start(r_tail[:], r_units[u]).then_inc(rt_loaded, 16)
                    if more(u):
                        load_weights(u + 2)

                def tail_last():
                    store_residual(NU - 1)
                    sp.wait_ge(r_stored, 16 * (NPAIR + NU))

                units(sp.Fori, head0, body, tail_last)

            @block.scalar
            def _(act):
                def normalise(v):
                    act.wait_ge(hscal, 4 * v + 4)
                    act.wait_ge(rh_loaded, 16 * v + 16)
                    for t in range(CT):
                        ins = nc.scalar.activation(xn[:, t, :], r_head[:, t, :], ACT.Identity,
                                                   bias=h_nmr[:, t:t + 1], scale=h_rstd[:, t:t + 1])
                    ins.then_inc(xn_done, 1)

                def evict(v, q, k):
                    ps = HB[:, k % 2, :]
                    act.wait_ge(hb_full, HEADS * v + k + 1)
                    if k < 2:
                        ins = nc.scalar.activation(hT[:, k, DC - 1:], ps, ACT.Identity,
                                                   bias=W[:, OLB:OLB + 1], scale=W[:, OLW:OLW + 1])
                    elif k < 10:
                        b, what = (k - 2) // 4, (k - 2) % 4
                        dst = (zs, xc)[what // 2][:, q, what % 2, b * L:(b + 1) * L]
                        ins = nc.scalar.copy(dst, ps)
                    elif k < 12:
                        ins = nc.scalar.copy(dblT[:, (k - 10) * L:(k - 9) * L], ps[0:NX])
                    else:
                        b, h = (k - 12) // 2, (k - 12) % 2
                        bias = W[:, ODB + h:ODB + h + 1]
                        cols = slice(b * L, (b + 1) * L)
                        nc.scalar.activation(dt[:, q, h, cols], ps, ACT.Relu, bias=bias)
                        ins = nc.scalar.activation(dtx[:, q, h, cols], ps, ACT.Abs, bias=bias)
                    ins.then_inc(hb_free, 1)

                def silus(v, q):
                    act.wait_ge(hb_free, 2 + HEADS * v + 10)
                    for h in range(EH):
                        nc.scalar.activation(xc[:, q, h, :], xc[:, q, h, :], ACT.Silu,
                                             bias=W[:, OCB + h:OCB + h + 1])
                    nc.scalar.activation(zs[:, q], zs[:, q], ACT.Silu).then_inc(silu_done, 1)

                def store_bc(v, q):
                    act.wait_ge(hb_free, 2 + HEADS * v + 12)
                    act.dma_start(bc_dram[q], dblT[RK:NX, :]).then_inc(bc_stored, 16)

                def log_part(v, q):
                    act.wait_ge(hb_free, 2 + HEADS * v + HEADS)
                    nc.scalar.activation(dtx[:, q], dtx[:, q], ACT.Exp, scale=-1.0).then_inc(exp_done, 1)
                    act.wait_ge(exp_done, v + 1)
                    act.wait_ge(dt_ready, v)
                    nc.scalar.activation(ln_u[:], dtx[:, q], ACT.Ln, bias=1.0).then_inc(ln_done, 1)

                def head_piece(n, v, q, tail):
                    if n == 0:
                        normalise(v)
                    if n == 1:
                        act.wait_ge(w_loaded, 16 * v + 16)
                    if n == 4 and tail:
                        act.wait_ge(yb_ready, v - 1)
                    for k in EVICT_AT.get(n, ()):
                        if k == 10:
                            act.wait_ge(bc_stored, 16 * v)
                        evict(v, q, k)
                    if n == 9:
                        silus(v, q)
                    if n == 11:
                        store_bc(v, q)
                    if n == 13:
                        log_part(v, q)

                def head0():
                    act.sem_inc(hb_free, 2)
                    act.wait_ge(zero_pads, 2)
                    for n in range(NST):
                        head_piece(n, 0, 0, False)

                def body(u, par, tail, head):
                    act.wait_ge(dt_ready, u + 1)
                    act.wait_ge(late_loaded, 16 * u + 16)
                    for n in range(NST):
                        act.wait_ge(scanned, EH * (NST * u + n + 1))
                        for h in range(EH):
                            a = OA + h * NST + n
                            ins = nc.scalar.activation(
                                dA[:, n % 2, h, :, 1:], dt[:, par, h, :].rearrange("p (b t) -> p b t", b=2)[:, :, 1:],
                                ACT.Exp, scale=late[:, par, a:a + 1])
                        ins.then_inc(dA_ready, 1)
                        if head:
                            head_piece(n, u + 1, 1 - par, tail)

                units(act.Fori, head0, body, lambda: None)

            @block.vector
            def _(dve):
                v_ = nc.vector

                def statistics(v):
                    dve.wait_ge(rh_loaded, 16 * v + 16)
                    for t in range(CT):
                        ins = v_.bn_stats(hstat[:, t, :], r_head[:, t, :])
                    ins.then_inc(hst_done, 1)
                    own_wait(dve, spare_d, hst_done, v + 1)
                    own_wait(dve, spare_d, hscal, 4 * v)
                    for t in range(CT):
                        ins = v_.bn_aggr(hmv[:, t, :], hstat[:, t, :])
                    ins.then_inc(hmv_ready, 1)

                def head_piece(n, v, q, tail):
                    if n == 13:
                        dve.wait_ge(exp_done, v + 1)
                        if tail:
                            dve.wait_ge(out_ready, 2 * v - 2)
                        v_.tensor_scalar(yb[:], dtx[:, q], 1.0, -1.0, ALU.add, ALU.add).then_inc(one_u, 1)
                        dve.wait_ge(ln_done, v + 1)
                        own_wait(dve, spare_d, one_u, v + 1)
                        v_.scalar_tensor_tensor(ln_u[:], yb[:], 0.0, ln_u[:], ALU.is_gt, ALU.mult
                                                ).then_inc(ln_exact, 1)
                        dve.wait_ge(ln_exact, v + 1)
                        v_.tensor_tensor(dt[:, q], dt[:, q], ln_u[:], ALU.add).then_inc(dt_half, 1)
                    if n == 14:
                        dve.wait_ge(lost_ready, v + 1)
                        dve.wait_ge(dt_half, v + 1)
                        v_.tensor_tensor(dt[:, q], dt[:, q], yb[:], ALU.add).then_inc(dt_ready, 1)
                    if n == 15:
                        dve.wait_ge(dt_ready, v + 1)
                        v_.tensor_tensor(dtx[:, q], dt[:, q], xc[:, q], ALU.mult).then_inc(dtx_ready, 1)

                def gate(v, q):
                    dve.wait_ge(reduced, RING + NST * v + NST)
                    own_wait(dve, spare_d, out_ready, 2 * v)
                    v_.tensor_tensor(yb[:], Y[:], zs[:, q], ALU.mult).then_inc(yb_ready, 1)

                def add_residual(v):
                    dve.wait_ge(rt_loaded, 16 * v + 16)
                    for i in range(2):
                        dve.wait_ge(out_ready, 2 * v + i + 1)
                        half = r_tail[:, 4 * i:4 * i + 4, :].rearrange("p t d -> p (t d)")
                        v_.tensor_tensor(half, half, HB[:, i, :], ALU.add).then_inc(r_ready, 1)

                def head0():
                    dve.sem_inc(dbu, EH * RING)
                    dve.sem_inc(g_dve, len(ON_DVE))
                    dve.sem_inc(scanned, 2 * EH)
                    v_.memset(hT[:, :, 0:DC - 1], 0.0).then_inc(zero_pads, 1)
                    v_.memset(dA[:, :, :, :, 0:1], 0.0).then_inc(zero_pads, 1)
                    statistics(0)
                    for n in range(NST):
                        head_piece(n, 0, 0, False)
                    statistics(1)

                def output_of_state(u, n):
                    s = n % RING
                    dve.wait_ge(C_loaded[s], 16 * (NST // RING) * u + 16 * (n // RING) + 16)
                    dve.wait_ge(scanned, EH * (2 + NST * u + n + 1))
                    v_.tensor_tensor(H[:, s], H[:, s], Cb[:, s, :].unsqueeze(1).to_broadcast([P, EH, U]),
                                     ALU.mult).then_inc(g_dve, 1)

                def body(u, par, tail, head):
                    own_wait(dve, spare_d, dtx_ready, u + 1)
                    for n in range(NST):
                        s = n % RING
                        dve.wait_ge(B_loaded[s], 16 * (NST // RING) * u + 16 * (n // RING) + 16)
                        for h in range(EH):
                            dve.wait_ge(scanned, EH * (2 + NST * u + n) + h)
                            v_.tensor_tensor(DBX[:], dtx[:, par, h, :], Bb[:, s, :], ALU.mult).then_inc(dbu, 1)
                            if h == 0 and n - 1 in ON_DVE:
                                output_of_state(u, n - 1)
                            if h == 0:
                                dve.wait_ge(reduced, NST * u + n + 1)
                                dve.wait_ge(dA_ready, NST * u + n + 1)
                            dve.wait_ge(dbu, EH * (RING + NST * u + n) + h + 1)
                            v_.tensor_tensor_scan(H[:, s, h, :], dA[:, n % 2, h].rearrange("p b t -> p (b t)"),
                                                  DBX[:], 0.0, ALU.mult, ALU.add).then_inc(scanned, 1)
                        if n == 1 and tail:
                            gate(u - 1, 1 - par)
                        if n == ADD_AT and tail:
                            add_residual(u - 1)
                        if head:
                            head_piece(n, u + 1, 1 - par, tail)
                        if n == 11 and more(u):
                            statistics(u + 2)
                    if NST - 1 in ON_DVE:
                        output_of_state(u, NST - 1)

                def tail_last():
                    gate(NU - 1, 1)
                    add_residual(NU - 1)

                units(dve.Fori, head0, body, tail_last)

            @block.gpsimd
            def _(pool):
                g_ = nc.gpsimd

                def norm_scalars(v):
                    own_wait(pool, spare_p, hmv_ready, v + 1)
                    own_wait(pool, spare_p, xn_done, v)
                    ch = Chain(pool, hscal, 4 * v)
                    ch.step(g_.tensor_scalar(h_ve[:], hmv[:, :, 1], EPS, None, ALU.add))
                    ch.step(g_.tensor_scalar(h_nm[:], hmv[:, :, 0], -1.0, None, ALU.mult))
                    ch.wait()
                    ch.step(g_.tensor_tensor(h_rstd[:], h_ve[:], neg_half[:, 0:CT], ALU.pow))
                    ch.wait()
                    ch.step(g_.tensor_tensor(h_nmr[:], h_nm[:], h_rstd[:], ALU.mult))

                def lost(v, q):
                    pool.wait_ge(ln_exact, v + 1)
                    g_.tensor_tensor(yb[:], dtx[:, q], yb[:], ALU.subtract).then_inc(lost_ready, 1)

                def head0():
                    pool.sem_inc(g_pool, len(ON_POOL))
                    norm_scalars(0)
                    lost(0, 0)
                    norm_scalars(1)

                def body(u, par, tail, head):
                    for n in ON_POOL:
                        if n == 14 and head:
                            lost(u + 1, 1 - par)
                        s = n % RING
                        pool.wait_ge(C_loaded[s], 16 * (NST // RING) * u + 16 * (n // RING) + 16)
                        pool.wait_ge(scanned, EH * (2 + NST * u + n + 1))
                        g_.tensor_tensor(H[:, s], H[:, s], Cb[:, s, :].unsqueeze(1).to_broadcast([P, EH, U]),
                                         ALU.mult).then_inc(g_pool, 1)
                        if n == 12 and more(u):
                            norm_scalars(u + 2)

                units(pool.Fori, head0, body, lambda: None)

            @block.tensor
            def _(pe):
                mm = nc.tensor.matmul

                def product(v, q, k):
                    pe.wait_ge(hb_free, HEADS * v + k + 1)
                    ps = HB[:, k % 2, :]
                    if k < 2:
                        for t in range(4):
                            ins = nc.tensor.transpose(ps[:, t * P:(t + 1) * P], xn[:, 4 * k + t, :], ident[:])
                    elif k < 10:
                        b, what = (k - 2) // 4, (k - 2) % 4
                        h = what % 2
                        if what < 2:
                            ins = mm(ps, W[:, OZ + h * P:OZ + (h + 1) * P], hT[:, b, DC - 1:], start=True, stop=True)
                        else:
                            for i in range(DC):
                                o = OTAP + i * DI + h * P
                                ins = mm(ps, W[:, o:o + P], hT[:, b, i:i + L], start=(i == 0), stop=(i == DC - 1))
                    elif k < 12:
                        b = k - 10
                        for h in range(EH):
                            o = OXP + h * NX
                            ins = mm(ps[0:NX], W[:, o:o + NX], xc[:, q, h, b * L:(b + 1) * L],
                                     start=(h == 0), stop=(h == EH - 1))
                    else:
                        b, h = (k - 12) // 2, (k - 12) % 2
                        o = ODT + h * P
                        ins = mm(ps, W[0:RK, o:o + P], dblT[0:RK, b * L:(b + 1) * L], start=True, stop=True)
                    ins.then_inc(hb_full, 1)

                def head_start(v, q):
                    pe.wait_ge(xn_done, v + 1)
                    product(v, q, 0)
                    product(v, q, 1)

                def head_piece(n, v, q, tail):
                    for k in MAKE_AT.get(n, ()):
                        if k == 2:
                            pe.wait_ge(w_loaded, 16 * v + 16)
                            pe.wait_ge(hb_free, 2 + HEADS * v + 2)
                        if k == 10:
                            pe.wait_ge(silu_done, v + 1)
                            if tail:
                                pe.wait_ge(r_ready, 2 * v - 2)
                        if k == 12:
                            pe.wait_ge(hb_free, 2 + HEADS * v + 12)
                        product(v, q, k)

                def project(v, q, in_psum):
                    pe.wait_ge(yb_ready, v + 1)
                    pe.wait_ge(hb_free, in_psum)
                    for i in range(2):
                        for t in range(4):
                            at = (4 * i + t) * P
                            for h in range(EH):
                                ins = mm(HB[:, i, t * D:(t + 1) * D], yb[:, h, at:at + P],
                                         late[:, q, OOW + h * D:OOW + (h + 1) * D],
                                         start=(h == 0), stop=(h == EH - 1))
                        ins.then_inc(out_ready, 1)

                def head0():
                    pe.sem_inc(reduced, RING)
                    pe.wait_ge(zero_pads, 2)
                    head_start(0, 0)
                    for n in range(NST):
                        head_piece(n, 0, 0, False)

                def body(u, par, tail, head):
                    if head:
                        head_start(u + 1, 1 - par)
                    for n in range(NST):
                        if n == 0:
                            pe.wait_ge(late_loaded, 16 * u + 16)
                            if tail:
                                pe.wait_ge(yb_ready, u)
                            for h in range(EH):
                                for b in range(2):
                                    cols = slice(b * L, (b + 1) * L)
                                    mm(Y[:, h, cols], late[:, par, ODG + h * P:ODG + (h + 1) * P],
                                       xc[:, par, h, cols], start=True, stop=False)
                        pe.wait_ge(*h_times_c(u, n))
                        for h in range(EH):
                            for b in range(2):
                                cols = slice(b * L, (b + 1) * L)
                                ins = mm(Y[:, h, cols], ident[:], H[:, n % RING, h, cols],
                                         start=False, stop=(n == NST - 1))
                        ins.then_inc(reduced, 1)
                        if n == PROJECT_AT and tail:
                            project(u - 1, 1 - par, 2 + HEADS * (u + 1) + (10 if head else 0))
                        if head:
                            head_piece(n, u + 1, 1 - par, tail)

                def tail_last():
                    pe.wait_ge(r_ready, 2 * NU - 2)
                    project(NU - 1, 1, 2 + HEADS * NU)

                units(pe.Fori, head0, body, tail_last)


def build(nc, io, out, L):
    T, D = io["x"].shape
    E, _, F = io["w1"].shape
    CAP = -(-T * 2 * 12 // (E * 10))
    xe_dram = [nc.dram_tensor(f"xe_slots{i}", (E * CAP, D + 1), F32).ap() for i in range(2)]
    y_rows = nc.dram_tensor("y_rows", (2 * T, D), F32).ap()
    x1_dram = nc.dram_tensor("x1", (T, D), F32).ap()
    r_dram = nc.dram_tensor("r", (3, T, D), F32).ap()
    w = {k: io[k] for k in ("gate_w", "gate_b", "w1", "b1", "w2", "b2")}
    with ExitStack() as ctx:
        def sb(name, shape, dt=F32):
            return ctx.enter_context(nc.sbuf_tensor(name, shape, dt))

        taken = []

        def sem(name):
            taken.append(nc.alloc_semaphore(name))
            return taken[-1]

        def stage_over():
            nc.clear_and_free_semaphores(taken)
            taken.clear()
            nc.all_engine_barrier()

        consts = (sb("ident", [P, P]), sb("ones_b", [P, P], BF16), sb("neg_tri", [P, P], BF16),
                  sb("rev", [P, E]), sb("not_first", [P, E, 8]), sb("neg_half", [P, T // P]),
                  sb("rev_i", [P, E], I32))
        emit_consts(nc, consts, sem)
        packs = Packs(nc, D, io)
        emit_moe(nc, 0, T, E, CAP, F, io["x"], None, x1_dram, r_dram[0], w, (xe_dram, y_rows), consts, sem, packs)
        stage_over()
        emit_attention(nc, T, L, D, packs, r_dram, consts, sem)
        stage_over()
        emit_moe(nc, 1, T, E, CAP, F, x1_dram, (r_dram[2], io["norm_w"], io["norm_b"]), out, None, w,
                 (xe_dram, y_rows), consts, sem)


def attention_layout(a, host):
    import numpy as np
    g = {k[len("L0_attn_"):]: v for k, v in a.items() if k.startswith("L0_attn_")}
    NL, E2, D = g["in_proj_w"].shape
    DI = E2 // 2
    EH = DI // P
    NX = g["x_proj_w"].shape[1]
    RK = g["dt_proj_w"].shape[2]

    def halves(m):
        c = m.reshape(NL, DI, -1).shape[2]
        return m.reshape(NL, EH, P, c).transpose(0, 2, 1, 3).reshape(NL, P, EH * c)

    in_T = g["in_proj_w"].transpose(0, 2, 1)
    dt_T = np.zeros((NL, P, DI), np.float32)
    dt_T[:, :RK] = g["dt_proj_w"].transpose(0, 2, 1)
    host["wpack"] = np.concatenate(
        [in_T[:, :, DI:], halves(g["x_proj_w"].transpose(0, 2, 1)), dt_T, g["ln_w"][:, :, None],
         g["ln_b"][:, :, None], halves(g["conv_b"]), halves(g["dt_proj_b"])], axis=2)
    host["late"] = np.concatenate(
        [halves(g["out_proj_w"].transpose(0, 2, 1)), halves(g["A_log"]), halves(g["D_skip"])], axis=2)
    host["in_x"] = in_T[:, :, :DI]
    host["conv_w"] = g["conv_w"].transpose(0, 2, 1)


def kernel(**inputs):
    import numpy as np
    import concourse.bacc as bacc
    from concourse.bass_utils import run_bass_kernel_spmd

    a = {k: np.asarray(v) for k, v in inputs.items()}
    B, S, D = a["L0_attn_x"].shape
    T = B * S
    E, _, F = a["L0_ffn_w1"].shape
    KF = F // P
    host = {
        "x": a["L0_attn_x"].reshape(T, D),
        "gate_w": a["L0_ffn_gate_w"], "gate_b": a["L0_ffn_gate_b"],
        "w1": a["L0_ffn_w1"], "w2": a["L0_ffn_w2"], "b2": a["L0_ffn_b2"],
        "b1": a["L0_ffn_b1"].reshape(E * KF, P).transpose(1, 0),
        "norm_w": a["L0_attn_norm_f_w"], "norm_b": a["L0_attn_norm_f_b"],
    }
    attention_layout(a, host)
    nc = bacc.Bacc("TRN2", target_bir_lowering=False, num_devices=1)
    arrays, io = {}, {}
    for name, v in host.items():
        v = np.ascontiguousarray(v)
        arrays[f"in_{name}"] = v
        io[name] = nc.dram_tensor(f"in_{name}", v.shape, mybir.dt.from_np(v.dtype), kind="ExternalInput").ap()
    out = nc.dram_tensor("out_0", (T, D), F32, kind="ExternalOutput").ap()
    build(nc, io, out, S)
    res = run_bass_kernel_spmd(nc, [arrays], core_ids=[0])
    return res.results[0]["out_0"].reshape(B, S, D)
```
